# Optimizing a Trainium2 kernel written in Bass

```python
import numpy as np
import jax
import jax.numpy as jnp

def _softmax(x, axis=-1):
    return jax.nn.softmax(x, axis=axis)

def _gelu(x):
    return jax.nn.gelu(x, approximate=True)

def _silu(x):
    return jax.nn.silu(x)

def _sigmoid(x):
    return jax.nn.sigmoid(x)

def _layernorm(x, axis=-1, eps=1e-05):
    m = jnp.mean(x, axis=axis, keepdims=True)
    v = jnp.var(x, axis=axis, keepdims=True)
    return (x - m) / jnp.sqrt(v + eps)

def _scatter_add(tgt, idx, src, axis=0):
    return tgt.at[idx].add(src)

def _segment_sum(src, seg, n):
    return jax.ops.segment_sum(src, seg, n)
kernel_name = 'mk_prb_d1_jaxref_r4_561d0a'

def setup_inputs(seed: int=0):
    np.random.seed(seed)
    _w = jnp.asarray

    def _L0_attn_setup():
        import jax, jax.numpy as jnp
        import numpy as np
        B, S, D, H = (2, 256, 256, 16)
        DK = D // H
        DE = D // 8
        SCALE = 1.0 / float(np.sqrt(DK))

        def _reference_tuple_inner(X, Wq, Wk, Wv, Wo, We):
            b, s, d = X.shape
            h, dk = (H, d // H)
            ctx = X @ We.T
            influence = jnp.einsum('bqe,bke->bqk', ctx, ctx)

            def heads(W):
                return (X @ W.T).reshape(b, s, h, dk).transpose(0, 2, 1, 3)
            Q, K, V = (heads(Wq), heads(Wk), heads(Wv))
            scores = jnp.einsum('bhqd,bhkd->bhqk', Q, K) * SCALE + 0.1 * influence[:, None]
            attn = jax.nn.softmax(scores, axis=-1)
            out = jnp.einsum('bhqk,bhkd->bhqd', attn, V)
            out = out.transpose(0, 2, 1, 3).reshape(b, s, d) @ Wo.T
            return (out, attn)
        key = jax.random.key(seed)
        ks = jax.random.split(key, 6)
        p = lambda k, shape: jax.random.normal(k, shape, dtype=jnp.float32) * 0.02
        return {'X': jax.random.normal(ks[0], (B, S, D), dtype=jnp.float32), 'Wq': p(ks[1], (D, D)), 'Wk': p(ks[2], (D, D)), 'Wv': p(ks[3], (D, D)), 'Wo': p(ks[4], (D, D)), 'We': p(ks[5], (DE, D))}
    _L0_attn_in = _L0_attn_setup()

    def _L0_ffn_setup():
        import jax, jax.numpy as jnp
        import numpy as np
        DIM = 256

        def _reference_tuple_inner(x, W_r, W_k, W_v, mu_r, mu_k):
            B, T, C = x.shape
            x_prev = jnp.concatenate([jnp.zeros((B, 1, C), x.dtype), x[:, :-1, :]], axis=1)
            xr = mu_r * x + (1.0 - mu_r) * x_prev
            xk = mu_k * x + (1.0 - mu_k) * x_prev
            r = jax.nn.sigmoid(jnp.einsum('btc,dc->btd', xr, W_r))
            k = jnp.einsum('btc,dc->btd', xk, W_k)
            k_act = jnp.square(jax.nn.relu(k))
            out = r * jnp.einsum('btc,dc->btd', k_act, W_v)
            new_state = x[:, -1, :]
            return (out, new_state)
        key = jax.random.key(seed)
        ks = jax.random.split(key, 6)
        B, T, C = (8, 512, DIM)
        x = jax.random.normal(ks[0], (B, T, C), dtype=jnp.float32)
        s = 1.0 / np.sqrt(C)
        W_r = jax.random.uniform(ks[1], (C, C), jnp.float32, -s, s)
        W_k = jax.random.uniform(ks[2], (C, C), jnp.float32, -s, s)
        W_v = jax.random.uniform(ks[3], (C, C), jnp.float32, -s, s)
        mu_r = jax.random.uniform(ks[4], (C,), jnp.float32)
        mu_k = jax.random.uniform(ks[5], (C,), jnp.float32)
        return {'x': x, 'W_r': W_r, 'W_k': W_k, 'W_v': W_v, 'mu_r': mu_r, 'mu_k': mu_k}
    _L0_ffn_in = _L0_ffn_setup()
    _d = {'L0_attn_X': _L0_attn_in['X'], 'L0_attn_Wq': _L0_attn_in['Wq'], 'L0_attn_Wk': _L0_attn_in['Wk'], 'L0_attn_Wv': _L0_attn_in['Wv'], 'L0_attn_Wo': _L0_attn_in['Wo'], 'L0_attn_We': _L0_attn_in['We'], 'L0_ffn_W_r': _L0_ffn_in['W_r'], 'L0_ffn_W_k': _L0_ffn_in['W_k'], 'L0_ffn_W_v': _L0_ffn_in['W_v'], 'L0_ffn_mu_r': _L0_ffn_in['mu_r'], 'L0_ffn_mu_k': _L0_ffn_in['mu_k']}
    _x0 = _d['L0_attn_X']
    _d['L0_attn_X'] = jax.random.normal(jax.random.fold_in(jax.random.key(seed), 1), (8, 512, 256), dtype=_x0.dtype)
    del _x0
    return _d

def reference(L0_attn_X, L0_attn_Wq, L0_attn_Wk, L0_attn_Wv, L0_attn_Wo, L0_attn_We, L0_ffn_W_r, L0_ffn_W_k, L0_ffn_W_v, L0_ffn_mu_r, L0_ffn_mu_k):

    def _L0_attn_ref(X, Wq, Wk, Wv, Wo, We):
        import jax, jax.numpy as jnp
        import numpy as np
        B, S, D, H = (2, 256, 256, 16)
        DK = D // H
        DE = D // 8
        SCALE = 1.0 / float(np.sqrt(DK))

        def _reference_tuple_inner(X, Wq, Wk, Wv, Wo, We):
            b, s, d = X.shape
            h, dk = (H, d // H)
            ctx = X @ We.T
            influence = jnp.einsum('bqe,bke->bqk', ctx, ctx)

            def heads(W):
                return (X @ W.T).reshape(b, s, h, dk).transpose(0, 2, 1, 3)
            Q, K, V = (heads(Wq), heads(Wk), heads(Wv))
            scores = jnp.einsum('bhqd,bhkd->bhqk', Q, K) * SCALE + 0.1 * influence[:, None]
            attn = jax.nn.softmax(scores, axis=-1)
            out = jnp.einsum('bhqk,bhkd->bhqd', attn, V)
            out = out.transpose(0, 2, 1, 3).reshape(b, s, d) @ Wo.T
            return (out, attn)
        return _reference_tuple_inner(X, Wq, Wk, Wv, Wo, We)[0]

    def _L0_ffn_ref(x, W_r, W_k, W_v, mu_r, mu_k):
        import jax, jax.numpy as jnp
        import numpy as np
        DIM = 256

        def _reference_tuple_inner(x, W_r, W_k, W_v, mu_r, mu_k):
            B, T, C = x.shape
            x_prev = jnp.concatenate([jnp.zeros((B, 1, C), x.dtype), x[:, :-1, :]], axis=1)
            xr = mu_r * x + (1.0 - mu_r) * x_prev
            xk = mu_k * x + (1.0 - mu_k) * x_prev
            r = jax.nn.sigmoid(jnp.einsum('btc,dc->btd', xr, W_r))
            k = jnp.einsum('btc,dc->btd', xk, W_k)
            k_act = jnp.square(jax.nn.relu(k))
            out = r * jnp.einsum('btc,dc->btd', k_act, W_v)
            new_state = x[:, -1, :]
            return (out, new_state)
        return _reference_tuple_inner(x, W_r, W_k, W_v, mu_r, mu_k)[0]
    x = L0_attn_X
    xn = _layernorm(x, axis=-1)
    x = x + _L0_attn_ref(xn, L0_attn_Wq, L0_attn_Wk, L0_attn_Wv, L0_attn_Wo, L0_attn_We) + _L0_ffn_ref(xn, L0_ffn_W_r, L0_ffn_W_k, L0_ffn_W_v, L0_ffn_mu_r, L0_ffn_mu_k)
    return x

_drawn_inputs = setup_inputs


def setup_inputs(seed=0):
    import zlib

    import numpy as np

    out = dict(_drawn_inputs(seed))
    spreads = {}
    factors = {'L0_attn_Wq': 8.0,
     'L0_attn_Wk': 8.0,
     'L0_attn_Wv': 8.0,
     'L0_attn_Wo': 8.0,
     'L0_attn_We': 8.0,
     'L0_ffn_W_r': 14.019,
     'L0_ffn_mu_r': 42.255,
     'L0_ffn_W_k': 3.24,
     'L0_ffn_W_v': 2.973,
     'L0_ffn_mu_k': 5.376}
    for name, (base, spread) in spreads.items():
        noise = np.random.default_rng([zlib.crc32(name.encode()), seed]).standard_normal(out[name].shape)
        drawn = base * np.exp(spread * noise) if base else spread * noise
        out[name] = jnp.asarray(drawn.astype(out[name].dtype))
    for name, factor in factors.items():
        out[name] = (out[name] * factor).astype(out[name].dtype)
    return out
```

```python
from contextlib import ExitStack

import concourse.bass as bass
from concourse import mybir

F32 = mybir.dt.float32
F32R = mybir.dt.float32r
ALU = mybir.AluOpType
ACT = mybir.ActivationFunctionType
AX = mybir.AxisListType

P = 128
B, S, D = 8, 512, 256
H, DK, DE = 16, 16, 32
CT = D // P
TT = S // P
HQ = 4
NQ = H // HQ
NU = NQ * TT
PIECES = HQ * TT
MAX_PLAN = [range(0, 6), range(6, 12), range(12, 16), range(0)]
SCALE = float(DK) ** -0.5
INFLUENCE = 0.1
EPS = 1e-5
ROW_Q = 32
ROW_QK2 = ROW_Q + DK
ROW_LOW = ROW_QK2 + DK
ROW_SHIFT = ROW_LOW + DK
ROWS = 97
SLOT_DMAS = 8 * 16
CA_DMAS = 2 * 16
O_DMAS = 2 * HQ * 16


def block_kernel(nc, x, wq, wk, wv, wo, we, wr, wkf, wvf, mu, out):
    ctx = ExitStack()
    with ctx:
        def sb(name, shape, dt=F32):
            return ctx.enter_context(nc.sbuf_tensor(name, shape, dt))

        def ps(name, shape):
            return ctx.enter_context(nc.psum_tensor(name, shape, F32))

        def sem(name):
            return ctx.enter_context(nc.semaphore(name))

        def raw(ap):
            return ap.bitcast(F32)

        QS = sb("q_operands", [P, H, S], F32R)
        KS = sb("k_operands", [P, H, S], F32R)
        CAQ = sb("context_q_operands", [P, 2, S], F32R)
        CAK = sb("context_k_operands", [P, 2, S], F32R)
        CTX = sb("context_staged", [P, S], F32R)
        PT = sb("probabilities", [P, 2, HQ, S])
        XT = sb("x_tokens", [P, TT, D])
        ACC = sb("sum_tokens", [P, TT, D])
        XN = sb("xn_tokens", [P, TT, D])
        KACT = XN[:, :, :].rearrange("p t d -> p (t d)").rearrange("p (c s) -> p c s", c=CT)
        XNT = sb("xn_channels", [P, CT, 1 + S])
        XNH = sb("xn_high", [P, CT, S], F32R)
        XNL = sb("xn_low", [P, CT, S], F32R)
        MIX = sb("mixed", [P, CT, S])
        MIXH = sb("mixed_high", [P, CT, S], F32R)
        MIXL = sb("mixed_low", [P, CT, S], F32R)
        LATEH = sb("kact_or_attn_high", [P, CT, S], F32R)
        LATEL = sb("kact_or_attn_low", [P, CT, S], F32R)
        QH = sb("q_high", [P, CT, S], F32R)
        QL = sb("q_low", [P, CT, S], F32R)
        KH = sb("k_high", [P, CT, S], F32R)
        KL = sb("k_low", [P, CT, S], F32R)
        VP = sb("values_and_ones", [P, TT, H, 2 * DK])
        OS = sb("attn_quarter", [P, 2, S])
        OT = sb("attn_channels", [P, CT, S])
        DEN = sb("attn_denominators", [P, CT, S])
        R = sb("gate", [P, TT, D])
        NEGM = sb("negated_maxima", [PIECES, P], F32R)
        MX = sb("maxima", [P, PIECES])
        IDENT = sb("identity", [P, P])
        STATS = sb("ln_stats", [P, TT, 6])
        MV = sb("ln_mean_var", [P, TT, 2])
        EPSV = sb("ln_eps", [P, TT])
        HALF = sb("ln_minus_half", [P, TT])
        VE = sb("ln_var_eps", [P, TT])
        RSTD = sb("ln_rstd", [P, TT])
        MU = sb("mu", [P, 2, CT])
        OMM = sb("one_minus_mu", [P, 2, CT])
        names = ["wq", "wk", "wv", "wo", "wr", "wkf", "wvf", "we"]
        width = {w: D for w in names} | {"we": P}
        WH = {w: sb(w + "_high", [P, CT, width[w]], F32R) for w in names}
        WL = {w: sb(w + "_low", [P, CT, width[w]], F32R) for w in names}
        w_dram = dict(wq=wq, wk=wk, wv=wv, wo=wo, wr=wr, wkf=wkf, wvf=wvf, we=we)
        flat = PT[:, :, :, :].rearrange("p a h s -> p (a h s)")
        WRAW, at = {}, 0
        for w in names:
            WRAW[w] = flat[:, at:at + CT * width[w]].rearrange("p (c n) -> p c n", c=CT)
            at += CT * width[w]

        MAXB = ps("scores_for_max", [P, 2, S])
        ST = [ps(f"scores_{i}", [P, 2, S]) for i in range(2)]
        PV = ps("attn_sums", [P, S])
        JOB = ps("job_sums", [P, S])
        JOB2 = JOB[:, :].rearrange("p (i d) -> p i d", i=2)

        w_loaded = sem("w_loaded")
        w_split = sem("w_split")
        w_high = sem("w_high")
        mu_ready = sem("mu_ready")
        zeroed = sem("zeroed")
        ident_zero = sem("ident_zero")
        ident_ready = sem("ident_ready")
        x_loaded = sem("x_loaded")
        stats_ready = sem("stats_ready")
        mv_ready = sem("mv_ready")
        var_ready = sem("var_ready")
        rstd_ready = sem("rstd_ready")
        xn_ready = sem("xn_ready")
        t_filled = sem("t_filled")
        xnt_ready = sem("xnt_ready")
        xn_high = sem("xn_high_ready")
        xn_split = sem("xn_split")
        qk_filled = sem("qk_filled")
        qk_high = sem("qk_high")
        qk_split = sem("qk_split")
        mix_scaled = sem("mix_scaled")
        mix_ready = sem("mix_ready")
        mix_high = sem("mix_high")
        mix_split = sem("mix_split")
        kf_filled = sem("kf_filled")
        relu_ready = sem("relu_ready")
        kact_ready = sem("kact_ready")
        kact_high = sem("kact_high")
        kact_split = sem("kact_split")
        ctx_filled = sem("ctx_filled")
        ctx_high = sem("ctx_high")
        ctx_staged = sem("ctx_staged")
        r_filled = sem("r_filled")
        r_ready = sem("r_ready")
        vf_filled = sem("vf_filled")
        vf_taken = sem("vf_taken")
        acc_loaded = sem("acc_loaded")
        acc_ready = sem("acc_ready")
        v_filled = sem("v_filled")
        v_ready = sem("v_ready")
        slot_loaded = [sem(f"slot_loaded{g}") for g in range(NQ)]
        ca_loaded = [sem(f"context_loaded{g}") for g in range(2)]
        max_filled = sem("max_filled")
        max_done = sem("max_done")
        shift_filled = sem("shift_filled")
        shift_taken = sem("shift_taken")
        shift_loaded = sem("shift_loaded")
        st_filled = [sem(f"scores_filled{i}") for i in range(2)]
        exp_done = [sem(f"exp_done{i}") for i in range(2)]
        pv_done = sem("pv_done")
        o_taken = sem("o_taken")
        o_loaded = [sem(f"o_loaded{i}") for i in range(2)]
        den_ready = sem("den_ready")
        o_normed = sem("o_normed")
        o_high = sem("o_high")
        o_split = sem("o_split")
        wo_filled = sem("wo_filled")
        out_ready = sem("out_ready")
        stored = sem("stored")

        block = ctx.enter_context(nc.Block())

        def run(eng, body):
            body(0, False, True)
            with eng.Fori(1, B - 1) as b:
                body(b, True, True)
            body(B - 1, True, False)

        @block.sync
        def _(sp):
            wait_values = [sp.alloc_register(f"wait_value{i}") for i in range(3)]

            def waits(*all_of):
                values = []
                for (_, v), r in zip(all_of, wait_values):
                    if not isinstance(v, int):
                        sp.reg_mov(r, v)
                        v = sp.snap(r)
                    values.append(v)
                for (s, _), v in zip(all_of, values):
                    sp.wait_ge(s, v)

            def load_x(n):
                sp.dma_start(XT[:, :, :], x[bass.ds(n, 1)].rearrange("o (t p) d -> p (o t) d", p=P)
                             ).then_inc(x_loaded, 16)

            def load_acc(b):
                sp.dma_start(ACC[:, :, :], x[bass.ds(b, 1)].rearrange("o (t p) d -> p (o t) d", p=P)
                             ).then_inc(acc_loaded, 16)

            def load_head_rows(n, g):
                waits((qk_split, 4 * n + 2 * (g // 2) + 2))
                src = slice(64 * (g % 2), 64 * (g % 2) + 64)
                h4 = slice(HQ * g, HQ * g + HQ)
                for dst, row, t in ((QS, ROW_Q, QH), (QS, ROW_QK2, QH), (QS, ROW_LOW, QL),
                                    (KS, ROW_Q, KH), (KS, ROW_QK2, KL), (KS, ROW_LOW, KH)):
                    sp.dma_start(raw(dst[row:row + DK, h4, :]),
                                 raw(t[src, g // 2, :])).then_inc(slot_loaded[g], 16)

            def load_context_rows(n, g):
                waits((ctx_staged, n + 1))
                h4 = slice(HQ * g, HQ * g + HQ)
                for dst, r0 in ((QS, 0), (KS, 3 * DE)):
                    src = raw(CTX[r0:r0 + DE, :]).rearrange("p (o s) -> p o s", o=1)
                    sp.dma_start(raw(dst[0:DE, h4, :]),
                                 src.broadcast_to([DE, HQ, S])).then_inc(slot_loaded[g], 16)

            def load_context_operands(n, g, *more):
                waits((ctx_staged, n + 1), *more)
                sp.dma_start(raw(CAQ[0:2 * DE, g % 2, :]), raw(CTX[0:2 * DE, :])).then_inc(ca_loaded[g % 2], 16)
                sp.dma_start(raw(CAK[0:2 * DE, g % 2, :]), raw(CTX[2 * DE:P, :])).then_inc(ca_loaded[g % 2], 16)

            def load_shift(q_after, g, *more):
                waits((shift_taken, q_after), *more)
                sp.dma_start(raw(QS[ROW_SHIFT:ROW_SHIFT + 1, HQ * g:HQ * g + HQ, :]),
                             raw(NEGM[:, :])).then_inc(shift_loaded, 16)

            def load_attn(b, g, *more):
                waits((o_taken, 4 * b + g + 1), (o_split, 2 * b), *more)
                for j in range(HQ):
                    dst = slice(64 * (g % 2) + DK * j, 64 * (g % 2) + DK * j + DK)
                    for t, r0 in ((OT, 0), (DEN, DK)):
                        sp.dma_start(t[dst, g // 2, :], OS[32 * j + r0:32 * j + r0 + DK, g % 2, :]
                                     ).then_inc(o_loaded[g // 2], 16)

            def store(b):
                sp.dma_start(out[bass.ds(b, 1)].rearrange("o (t p) d -> p (o t) d", p=P), ACC[:, :, :]
                             ).then_inc(stored, 16)

            def scores_read(count):
                return st_filled[1], count

            sp.dma_start(XT[:, :, :], x[0].rearrange("(t p) d -> p t d", p=P)).then_inc(x_loaded, 16)
            for w in names:
                src = w_dram[w].rearrange("(c p) n -> p c n", p=P)
                if w == "we":
                    for r in range(4):
                        sp.dma_start(WRAW[w][:, :, DE * r:DE * r + DE], src).then_inc(w_loaded, 16)
                else:
                    sp.dma_start(WRAW[w], src).then_inc(w_loaded, 16)
            sp.dma_start(MU[:, :, :], mu).then_inc(w_loaded, 16)
            sp.wait_ge(zeroed, 2)
            for g in range(3):
                load_head_rows(0, g)
            load_context_operands(0, 0)
            for g in range(3):
                load_context_rows(0, g)
            load_shift(1, 0)

            def body(b, has_prev, has_next):
                n = b + 1
                if has_prev:
                    load_attn(b - 1, 3, (xn_ready, n))
                if has_next:
                    load_x(n)
                load_context_operands(b, 1, scores_read(16 * b))
                load_head_rows(b, 3)
                load_context_rows(b, 3)
                load_shift(4 * b + 2, 1)
                load_context_operands(b, 2, scores_read(16 * b + 4), (out_ready, 2 * b))
                if has_prev:
                    store(b - 1)
                load_attn(b, 0)
                load_shift(4 * b + 3, 2, (stored, 16 * b))
                load_acc(b)
                load_context_operands(b, 3, scores_read(16 * b + 8))
                if has_next:
                    load_head_rows(n, 0)
                    load_head_rows(n, 1)
                load_attn(b, 1)
                if has_next:
                    load_context_rows(n, 0)
                    load_context_rows(n, 1)
                load_shift(4 * b + 4, 3)
                if has_next:
                    load_context_operands(n, 0, scores_read(16 * b + 12))
                    load_head_rows(n, 2)
                    load_context_rows(n, 2)
                load_attn(b, 2)
                if has_next:
                    load_shift(4 * b + 5, 0)

            run(sp, body)
            load_attn(B - 1, 3)
            sp.wait_ge(out_ready, 2 * B)
            store(B - 1)
            sp.wait_ge(stored, 16 * B)

        @block.tensor
        def _(pe):
            mm = nc.tensor.matmul

            def product(dst, lhs, rhs):
                (lh, ll), (rh, rl) = lhs, rhs
                terms = [(a, c, k) for a, c in ((lh, rl), (ll, rh), (lh, rh)) for k in range(CT)]
                for i, (a, c, k) in enumerate(terms):
                    last = mm(dst, a(k), c(k), start=(i == 0), stop=(i == len(terms) - 1))
                return last

            def pair(high, low, cols):
                return (lambda k: high[:, k, cols]), (lambda k: low[:, k, cols])

            def cols(i, n=P):
                return slice(i * n, i * n + n)

            every = slice(None)

            def job_transpose(n):
                pe.wait_ge(xn_ready, n + 1)
                for j in range(CT):
                    if j == 0:
                        pe.wait_ge(v_ready, 2 * n)
                    else:
                        pe.wait_ge(xnt_ready, 2 * n + 1)
                    for t in range(TT):
                        last = nc.tensor.transpose(JOB[:, cols(t)], XN[:, t, cols(j)], IDENT[:, :])
                    last.then_inc(t_filled, 1)

            def job_out(b):
                pe.wait_ge(o_split, 2 * b + 2)
                for j in range(2):
                    if j == 1:
                        pe.wait_ge(out_ready, 2 * b + 1)
                    for i in range(2):
                        last = product(JOB2[:, i, :], pair(LATEH, LATEL, cols(2 * j + i)),
                                       pair(WH["wo"], WL["wo"], every))
                    last.then_inc(wo_filled, 1)

            def job_qk(n, i):
                if i == 0:
                    pe.wait_ge(xn_split, n + 1)
                else:
                    pe.wait_ge(qk_split, 4 * n + i)
                w = ("wq", "wk")[i % 2]
                product(JOB[:, :], pair(WH[w], WL[w], cols(i // 2)), pair(XNH, XNL, every)
                        ).then_inc(qk_filled, 1)

            def job_kf(n):
                pe.wait_ge(qk_split, 4 * n + 4)
                pe.wait_ge(mix_split, 2 * n + 1)
                for j in range(CT):
                    if j == 1:
                        pe.wait_ge(relu_ready, 2 * n + 1)
                    product(JOB[:, :], pair(WH["wkf"], WL["wkf"], cols(j)), pair(MIXH, MIXL, every)
                            ).then_inc(kf_filled, 1)

            def job_context(n):
                pe.wait_ge(relu_ready, 2 * n + 2)
                product(JOB[:, :], pair(WH["we"], WL["we"], every), pair(XNH, XNL, every)
                        ).then_inc(ctx_filled, 1)

            def token_job(n, j, lhs, w, filled):
                for i in range(2):
                    last = product(JOB2[:, i, :], pair(*lhs, cols(2 * j + i)), pair(WH[w], WL[w], every))
                last.then_inc(filled, 1)

            def job_gate(n, j):
                if j == 0:
                    pe.wait_ge(ctx_staged, n + 1)
                    pe.wait_ge(mix_split, 2 * n + 2)
                else:
                    pe.wait_ge(r_ready, 2 * n + 1)
                token_job(n, j, (MIXH, MIXL), "wr", r_filled)

            def job_vf(n, j):
                if j == 0:
                    pe.wait_ge(r_ready, 2 * n + 2)
                    pe.wait_ge(kact_split, n + 1)
                else:
                    pe.wait_ge(vf_taken, 2 * n + 1)
                token_job(n, j, (LATEH, LATEL), "wvf", vf_filled)

            def job_v(n, j):
                if j == 0:
                    pe.wait_ge(vf_taken, 2 * n + 2)
                else:
                    pe.wait_ge(v_ready, 2 * n + 1)
                token_job(n, j, (XNH, XNL), "wv", v_filled)

            def max_piece(b, g, i):
                q = 4 * b + g
                if i == 0:
                    pe.wait_ge(slot_loaded[g], SLOT_DMAS * (b + 1))
                    pe.wait_ge(shift_taken, q)
                elif i >= 2:
                    pe.wait_ge(max_done, PIECES * q + i - 1)
                h = HQ * g + i // TT
                mm(MAXB[:, i % 2, :], QS[0:ROW_QK2, h, cols(i % TT)], KS[0:ROW_QK2, h, :],
                   start=True, stop=True).then_inc(max_filled, 1)

            def shift_rows(b, g):
                pe.wait_ge(max_done, PIECES * (4 * b + g + 1))
                nc.tensor.transpose(MAXB[0:PIECES, 0, 0:P], MX[:, :], IDENT[:, :]).then_inc(shift_filled, 1)

            def exact_scores(b, g, kt):
                u = 16 * b + 4 * g + kt
                if kt == 0:
                    pe.wait_ge(ca_loaded[g % 2], CA_DMAS * (2 * b + g // 2 + 1))
                    pe.wait_ge(shift_loaded, 16 * (4 * b + g + 1))
                for half in range(2):
                    pe.wait_ge(exp_done[half], u)
                    for j in range(2):
                        h = HQ * g + 2 * half + j
                        mm(ST[half][:, j, :], CAK[:, g % 2, cols(kt)], CAQ[:, g % 2, :],
                           start=True, stop=False)
                        last = mm(ST[half][:, j, :], KS[0:ROWS, h, cols(kt)], QS[0:ROWS, h, :],
                                  start=False, stop=True)
                    last.then_inc(st_filled[half], 1)

            def values(b, g, kt):
                u = 16 * b + 4 * g + kt
                if g == 0 and kt % 2 == 0:
                    pe.wait_ge(v_ready, 2 * b + kt // 2 + 1)
                if kt == 0:
                    pe.wait_ge(o_taken, 4 * b + g)
                for half in range(2):
                    pe.wait_ge(exp_done[half], u + 1)
                for j in range(HQ):
                    last = mm(PV[32 * j:32 * j + 32, :], VP[:, kt, HQ * g + j, :], PT[:, u_par(kt), j, :],
                              start=(kt == 0), stop=(kt == TT - 1))
                last.then_inc(pv_done, 1)

            def u_par(kt):
                return kt % 2

            pe.wait_ge(ident_ready, 1)
            pe.wait_ge(w_split, len(names))
            pe.wait_ge(zeroed, 4)
            job_transpose(0)
            for i in range(4):
                job_qk(0, i)
            job_kf(0)
            job_context(0)
            for j in range(2):
                job_gate(0, j)
            for j in range(2):
                job_vf(0, j)
            for j in range(2):
                job_v(0, j)
            for i in range(PIECES):
                max_piece(0, 0, i)
            shift_rows(0, 0)

            def body(b, has_prev, has_next):
                n = b + 1
                for u in range(NU):
                    g, kt = divmod(u, TT)
                    ahead = (b, g + 1) if g < NQ - 1 else (n, 0)
                    look = g < NQ - 1 or has_next
                    if look:
                        for i in MAX_PLAN[kt]:
                            max_piece(*ahead, i)
                    exact_scores(b, g, kt)
                    if u == 2 and has_next:
                        job_transpose(n)
                    if u == 3 and has_prev:
                        if has_next:
                            pe.wait_ge(xnt_ready, 2 * n + 2)
                        else:
                            pe.wait_ge(v_ready, 2 * b + 2)
                        job_out(b - 1)
                    if has_next:
                        if u == 4:
                            if has_prev:
                                pe.wait_ge(out_ready, 2 * b)
                            else:
                                pe.wait_ge(xnt_ready, 2 * n + 2)
                        if 4 <= u < 8:
                            job_qk(n, u - 4)
                        if u == 8:
                            job_kf(n)
                        if u == 9:
                            job_context(n)
                        if u == 10:
                            for j in range(2):
                                job_gate(n, j)
                        if 12 <= u < 14:
                            job_vf(n, u - 12)
                        if u == 14:
                            job_v(n, 0)
                    if u > 0:
                        values(b, (u - 1) // TT, (u - 1) % TT)
                    if look and kt == 2:
                        shift_rows(*ahead)
                if has_next:
                    job_v(n, 1)
                values(b, NQ - 1, TT - 1)

            run(pe, body)
            pe.wait_ge(out_ready, 2 * B - 2)
            job_out(B - 1)

        @block.scalar
        def _(act):
            A = nc.scalar.activation

            def exps(b, g, kt):
                u = 16 * b + 4 * g + kt
                if 4 * g + kt == 0:
                    act.wait_ge(pv_done, u)
                elif 4 * g + kt > 1:
                    act.wait_ge(pv_done, u - 1)
                for half in range(2):
                    act.wait_ge(st_filled[half], u + 1)
                    A(PT[:, kt % 2, 2 * half:2 * half + 2, :], ST[half][:, :, :], ACT.Exp
                      ).then_inc(exp_done[half], 1)

            def take_attn(b, g):
                act.wait_ge(pv_done, 16 * b + 4 * (g + 1))
                if g >= 2:
                    act.wait_ge(o_loaded[0], O_DMAS * (2 * b + 2))
                else:
                    act.wait_ge(o_loaded[1], O_DMAS * (2 * b))
                A(OS[:, g % 2, :], PV[:, :], ACT.Copy).then_inc(o_taken, 1)

            def take_transposes(n):
                act.wait_ge(mix_split, 2 * n)
                act.wait_ge(xn_split, n)
                for j in range(CT):
                    act.wait_ge(t_filled, 2 * n + j + 1)
                    A(XNT[:, j, 1:], JOB[:, :], ACT.Copy).then_inc(xnt_ready, 1)

            def scale_before(n, i):
                act.wait_ge(xnt_ready, 2 * n + 2)
                act.wait_ge(mix_split, 2 * n + i)
                for c in range(CT):
                    A(MIX[:, c, :], XNT[:, c, 0:S], ACT.Copy, scale=OMM[:, i, c:c + 1]
                      ).then_inc(mix_scaled, 1)

            def qk_highs(n, i):
                act.wait_ge(qk_filled, 4 * n + i + 1)
                if i == 0:
                    for g in range(NQ):
                        act.wait_ge(slot_loaded[g], SLOT_DMAS * n)
                A((QH, KH)[i % 2][:, i // 2, :], JOB[:, :], ACT.Copy, scale=(SCALE, 1.0)[i % 2]
                  ).then_inc(qk_high, 1)

            def relus(n, j):
                act.wait_ge(kf_filled, 2 * n + j + 1)
                act.wait_ge(t_filled, 2 * n + 2)
                A(KACT[:, j, :], JOB[:, :], ACT.Relu).then_inc(relu_ready, 1)

            def context_highs(n):
                act.wait_ge(ctx_filled, n + 1)
                for g in range(NQ):
                    act.wait_ge(slot_loaded[g], SLOT_DMAS * n)
                for i in range(2):
                    act.wait_ge(ca_loaded[i], CA_DMAS * 2 * n)
                A(CTX[0:2 * DE, :], JOB[0:2 * DE, :], ACT.Copy)
                A(CTX[2 * DE:P, :], JOB[2 * DE:P, :], ACT.Copy, scale=INFLUENCE).then_inc(ctx_high, 1)

            def gates(n, j):
                act.wait_ge(r_filled, 2 * n + j + 1)
                act.wait_ge(acc_ready, 2 * n)
                A(R[:, 2 * j:2 * j + 2, :], JOB2[:, :, :], ACT.Sigmoid).then_inc(r_ready, 1)

            def take_values(n, j, b=None):
                act.wait_ge(v_filled, 2 * n + j + 1)
                if b is not None:
                    act.wait_ge(pv_done, 16 * b + 14 + 2 * j)
                A(VP[:, 2 * j:2 * j + 2, :, 0:DK],
                  JOB2[:, :, :].rearrange("p i (h d) -> p i h d", h=H), ACT.Copy).then_inc(v_ready, 1)

            act.wait_ge(zeroed, 6)
            act.wait_ge(mu_ready, 1)
            take_transposes(0)
            scale_before(0, 0)
            for i in range(4):
                qk_highs(0, i)
            for j in range(2):
                relus(0, j)
            context_highs(0)
            scale_before(0, 1)
            for j in range(2):
                gates(0, j)
            for j in range(2):
                take_values(0, j)

            def body(b, has_prev, has_next):
                n = b + 1
                for u in range(NU):
                    g, kt = divmod(u, TT)
                    exps(b, g, kt)
                    if has_next:
                        if u == 2:
                            take_transposes(n)
                        if u == 3:
                            scale_before(n, 0)
                        if 4 <= u < 8:
                            qk_highs(n, u - 4)
                        if u == 8:
                            for j in range(2):
                                relus(n, j)
                        if u == 7:
                            scale_before(n, 1)
                        if u == 9:
                            context_highs(n)
                        if u == 10:
                            for j in range(2):
                                gates(n, j)
                        if u == 14:
                            take_values(n, 0, b)
                    if kt == 0 and g > 0:
                        take_attn(b, g - 1)
                if has_next:
                    take_values(n, 1, b)
                take_attn(b, NQ - 1)

            run(act, body)

        @block.vector
        def _(dve):
            V = nc.vector

            def row_maxima(b, g, pieces):
                for i in pieces:
                    dve.wait_ge(max_filled, PIECES * (4 * b + g) + i + 1)
                    V.reduce_max(MX[:, i:i + 1], MAXB[:, i % 2, :], AX.X).then_inc(max_done, 1)

            def take_shift(b, g):
                q = 4 * b + g
                dve.wait_ge(shift_filled, q + 1)
                dve.wait_ge(shift_loaded, 16 * q)
                V.tensor_scalar(NEGM[:, :], MAXB[0:PIECES, 0, 0:P], -1.0, None, ALU.mult
                                ).then_inc(shift_taken, 1)

            def layernorm_stats(n):
                dve.wait_ge(x_loaded, 16 * (n + 1))
                for t in range(TT):
                    last = V.bn_stats(STATS[:, t, :], XT[:, t, :])
                last.then_inc(stats_ready, 1)

            def layernorm_moments(n):
                for t in range(TT):
                    last = V.bn_aggr(MV[:, t, :], STATS[:, t, :])
                last.then_inc(mv_ready, 1)

            def layernorm(n):
                dve.wait_ge(rstd_ready, n + 1)
                dve.wait_ge(kact_split, n)
                for t in range(TT):
                    last = V.tensor_scalar(XN[:, t, :], XT[:, t, :], MV[:, t, 0:1], RSTD[:, t:t + 1],
                                           ALU.subtract, ALU.mult)
                last.then_inc(xn_ready, 1)

            def xn_highs(n):
                dve.wait_ge(xnt_ready, 2 * n + 2)
                dve.wait_ge(v_filled, 2 * n)
                V.tensor_copy(XNH[:, :, :], XNT[:, :, 1:]).then_inc(xn_high, 1)

            def qk_lows(n, i):
                dve.wait_ge(qk_high, 4 * n + i + 1)
                high, low = ((QH, QL), (KH, KL))[i % 2]
                V.scalar_tensor_tensor(out=low[:, i // 2, :], in0=JOB[:, :], scalar=(SCALE, 1.0)[i % 2],
                                       in1=raw(high[:, i // 2, :]), op0=ALU.mult, op1=ALU.subtract
                                       ).then_inc(qk_split, 1)

            def mix(n, i):
                for c in range(CT):
                    dve.wait_ge(mix_scaled, 4 * n + 2 * i + c + 1)
                    last = V.scalar_tensor_tensor(out=MIX[:, c, :], in0=XNT[:, c, 1:], scalar=MU[:, i, c:c + 1],
                                                  in1=MIX[:, c, :], op0=ALU.mult, op1=ALU.add)
                last.then_inc(mix_ready, 1)
                dve.wait_ge(mix_ready, 2 * n + i + 1)
                if i == 0:
                    dve.wait_ge(r_filled, 2 * n)
                else:
                    dve.wait_ge(kf_filled, 2 * n + 2)
                V.tensor_copy(MIXH[:, :, :], MIX[:, :, :]).then_inc(mix_high, 1)

            def kact_highs(n, b=None):
                dve.wait_ge(kact_ready, n + 1)
                if b is not None:
                    dve.wait_ge(wo_filled, 2 * b)
                V.tensor_copy(LATEH[:, :, :], KACT).then_inc(kact_high, 1)

            def context_lows(n):
                dve.wait_ge(ctx_high, n + 1)
                V.tensor_tensor(CTX[DE:2 * DE, :], JOB[DE:2 * DE, :], raw(CTX[DE:2 * DE, :]), ALU.subtract)
                V.scalar_tensor_tensor(out=CTX[2 * DE:3 * DE, :], in0=JOB[2 * DE:3 * DE, :], scalar=INFLUENCE,
                                       in1=raw(CTX[2 * DE:3 * DE, :]), op0=ALU.mult, op1=ALU.subtract
                                       ).then_inc(ctx_staged, 1)

            def take_vf(n, j):
                r = R[:, 2 * j:2 * j + 2, :]
                dve.wait_ge(vf_filled, 2 * n + j + 1)
                dve.wait_ge(r_ready, 2 * n + j + 1)
                V.tensor_tensor(r, JOB2[:, :, :], r, ALU.mult).then_inc(vf_taken, 1)

            def norm_attn(b, t):
                dve.wait_ge(o_loaded[t], O_DMAS * (2 * b + 2))
                V.reciprocal(DEN[:, t, :], DEN[:, t, :]).then_inc(den_ready, 1)
                dve.wait_ge(den_ready, 2 * b + t + 1)
                V.tensor_tensor(OT[:, t, :], OT[:, t, :], DEN[:, t, :], ALU.mult).then_inc(o_normed, 1)

            def attn_highs(b, t, n=None):
                dve.wait_ge(o_normed, 2 * b + t + 1)
                if n is not None:
                    dve.wait_ge(vf_filled, 2 * n + 2)
                elif t == 0:
                    dve.wait_ge(wo_filled, 2 * b)
                V.tensor_copy(LATEH[:, t, :], OT[:, t, :]).then_inc(o_high, 1)

            def take_out(b, j):
                acc = ACC[:, 2 * j:2 * j + 2, :]
                dve.wait_ge(wo_filled, 2 * b + j + 1)
                dve.wait_ge(acc_ready, 2 * b + 2)
                V.tensor_tensor(acc, JOB2[:, :, :], acc, ALU.add).then_inc(out_ready, 1)

            V.memset(raw(QS[64:P, :, :]), 0.0).then_inc(zeroed, 1)
            V.memset(raw(KS[64:P, :, :]), 1.0).then_inc(zeroed, 1)
            V.memset(raw(CAQ[2 * DE:P, :, :]), 0.0).then_inc(zeroed, 1)
            V.memset(raw(CAK[2 * DE:P, :, :]), 0.0).then_inc(zeroed, 1)
            V.memset(XNT[:, :, 0:1], 0.0).then_inc(zeroed, 1)
            V.memset(VP[:, :, :, :], 1.0).then_inc(zeroed, 1)
            layernorm_stats(0)
            dve.wait_ge(stats_ready, 1)
            layernorm_moments(0)
            dve.wait_ge(w_loaded, 16 * (len(names) + 3 + 1))
            V.tensor_scalar(OMM[:, :, :], MU[:, :, :], -1.0, 1.0, ALU.mult, ALU.add).then_inc(mu_ready, 1)
            for w in names:
                last = V.tensor_copy(WH[w][:, :, :], WRAW[w])
            last.then_inc(w_high, 1)
            dve.wait_ge(w_high, 1)
            for w in names:
                V.tensor_tensor(WL[w][:, :, :], WRAW[w], raw(WH[w][:, :, :]), ALU.subtract
                                ).then_inc(w_split, 1)
            layernorm(0)
            xn_highs(0)
            mix(0, 0)
            for i in range(4):
                qk_lows(0, i)
            kact_highs(0)
            context_lows(0)
            mix(0, 1)
            for j in range(2):
                take_vf(0, j)
            row_maxima(0, 0, range(PIECES))
            take_shift(0, 0)

            def body(b, has_prev, has_next):
                n = b + 1
                for u in range(NU):
                    g, kt = divmod(u, TT)
                    ahead = (b, g + 1) if g < NQ - 1 else (n, 0)
                    look = g < NQ - 1 or has_next
                    if has_next and u == 1:
                        dve.wait_ge(stats_ready, n + 1)
                    if look:
                        row_maxima(*ahead, MAX_PLAN[kt])
                    if has_next:
                        if u == 0:
                            layernorm_stats(n)
                        if u == 1:
                            layernorm_moments(n)
                    if has_prev and u == 1:
                        norm_attn(b - 1, 1)
                        attn_highs(b - 1, 1)
                    if has_next:
                        if u == 1:
                            layernorm(n)
                    if has_next and u == 2:
                        xn_highs(n)
                    if has_prev and u == 3:
                        for j in range(2):
                            take_out(b - 1, j)
                    if has_next:
                        if u == 4:
                            mix(n, 0)
                        if 4 <= u < 8:
                            qk_lows(n, u - 4)
                        if u == 9:
                            kact_highs(n, b if has_prev else None)
                            context_lows(n)
                            mix(n, 1)
                        if 12 <= u < 14:
                            take_vf(n, u - 12)
                    if u == 11:
                        norm_attn(b, 0)
                    if u == 14:
                        attn_highs(b, 0, n if has_next else None)
                    if look and kt == 2:
                        take_shift(*ahead)

            run(dve, body)
            norm_attn(B - 1, 1)
            attn_highs(B - 1, 1)
            for j in range(2):
                take_out(B - 1, j)

        @block.gpsimd
        def _(pool):
            G = nc.gpsimd

            def rstd(n):
                pool.wait_ge(mv_ready, n + 1)
                pool.wait_ge(xn_ready, n)
                G.tensor_tensor(VE[:, :], MV[:, :, 1], EPSV[:, :], ALU.add).then_inc(var_ready, 1)
                pool.wait_ge(var_ready, n + 1)
                G.tensor_tensor(RSTD[:, :], VE[:, :], HALF[:, :], ALU.pow).then_inc(rstd_ready, 1)

            def lows(ready, count, low, whole, high, done):
                pool.wait_ge(ready, count)
                G.tensor_tensor(low, whole, raw(high), ALU.subtract).then_inc(done, 1)

            def xn_lows(n):
                lows(xn_high, n + 1, XNL[:, :, :], XNT[:, :, 1:], XNH[:, :, :], xn_split)

            def mix_lows(n, i):
                lows(mix_high, 2 * n + i + 1, MIXL[:, :, :], MIX[:, :, :], MIXH[:, :, :], mix_split)

            def kacts(n):
                pool.wait_ge(relu_ready, 2 * n + 2)
                G.tensor_tensor(KACT, KACT, KACT, ALU.mult).then_inc(kact_ready, 1)

            def kact_lows(n):
                lows(kact_high, n + 1, LATEL[:, :, :], KACT, LATEH[:, :, :], kact_split)

            def attn_lows(b, t):
                lows(o_high, 2 * b + t + 1, LATEL[:, t, :], OT[:, t, :], LATEH[:, t, :], o_split)

            def add_vf(n, j):
                pool.wait_ge(vf_taken, 2 * n + j + 1)
                pool.wait_ge(acc_loaded, 16 * (n + 1))
                acc = ACC[:, 2 * j:2 * j + 2, :]
                G.tensor_tensor(acc, acc, R[:, 2 * j:2 * j + 2, :], ALU.add).then_inc(acc_ready, 1)

            G.memset(IDENT[:, :], 0.0).then_inc(ident_zero, 1)
            pool.wait_ge(ident_zero, 1)
            G.affine_select(out=IDENT[:, :], in_=IDENT[:, :], compare_op=ALU.not_equal, fill=1.0, base=0,
                            pattern=[[-1, P]], channel_multiplier=1).then_inc(ident_ready, 1)
            G.memset(EPSV[:, :], EPS).then_inc(ident_zero, 1)
            G.memset(HALF[:, :], -0.5).then_inc(ident_zero, 1)
            pool.wait_ge(ident_zero, 3)
            rstd(0)
            xn_lows(0)
            mix_lows(0, 0)
            kacts(0)
            kact_lows(0)
            mix_lows(0, 1)

            def body(b, has_prev, has_next):
                n = b + 1
                if has_next:
                    rstd(n)
                if has_prev:
                    attn_lows(b - 1, 1)
                if has_next:
                    xn_lows(n)
                    mix_lows(n, 0)
                for j in range(2):
                    add_vf(b, j)
                if has_next:
                    kacts(n)
                    kact_lows(n)
                    mix_lows(n, 1)
                attn_lows(b, 0)

            run(pool, body)
            attn_lows(B - 1, 1)


_INS = ["x", "wq", "wk", "wv", "wo", "we", "wr", "wkf", "wvf", "mu"]


def kernel(L0_attn_X, L0_attn_Wq, L0_attn_Wk, L0_attn_Wv, L0_attn_Wo, L0_attn_We,
           L0_ffn_W_r, L0_ffn_W_k, L0_ffn_W_v, L0_ffn_mu_r, L0_ffn_mu_k):
    import numpy as np
    import concourse.bacc as bacc
    from concourse.bass_utils import run_bass_kernel_spmd

    def by_channel(w):
        w = np.asarray(w).T.reshape(D, H // HQ, HQ, DK)
        return np.ascontiguousarray(w.transpose(0, 1, 3, 2).reshape(D, D))

    def turned(w):
        return np.ascontiguousarray(np.asarray(w).T)

    arrays = {
        "x": np.ascontiguousarray(L0_attn_X),
        "wq": by_channel(L0_attn_Wq), "wk": by_channel(L0_attn_Wk), "wv": turned(L0_attn_Wv),
        "wo": turned(L0_attn_Wo), "we": turned(L0_attn_We), "wr": turned(L0_ffn_W_r),
        "wkf": turned(L0_ffn_W_k), "wvf": turned(L0_ffn_W_v),
        "mu": np.ascontiguousarray(np.stack([L0_ffn_mu_k, L0_ffn_mu_r]).reshape(2, CT, P).transpose(2, 0, 1)),
    }
    nc = bacc.Bacc("TRN2", target_bir_lowering=False, num_devices=1)
    args = [nc.dram_tensor(f"in_{k}", arrays[k].shape, mybir.dt.from_np(arrays[k].dtype),
                           kind="ExternalInput").ap() for k in _INS]
    out = nc.dram_tensor("out_0", (B, S, D), F32, kind="ExternalOutput").ap()
    block_kernel(nc, *args, out)
    r = run_bass_kernel_spmd(nc, [{f"in_{k}": arrays[k] for k in _INS}], core_ids=[0])
    return r.results[0]["out_0"]
```

```python
from contextlib import ExitStack

import concourse.bass as bass
from concourse import mybir

F32 = mybir.dt.float32
F32R = mybir.dt.float32r
ALU = mybir.AluOpType
ACT = mybir.ActivationFunctionType
AX = mybir.AxisListType

P = 128
B, S, D = 8, 512, 256
H, DK, DE = 16, 16, 32
CT = D // P
TT = S // P
HQ = 4
NQ = H // HQ
NU = NQ * TT
PIECES = HQ * TT
BANK_USES = PIECES + 1
SCALE = float(DK) ** -0.5
INFLUENCE = 0.1
EPS = 1e-5
ROW_Q = 32
ROW_QK2 = ROW_Q + DK
ROW_LOW = ROW_QK2 + DK
ROW_SHIFT = ROW_LOW + DK
ROWS = 97
HEAD_DMAS = 6 * 16
CA_DMAS = 2 * 16
O_DMAS = 2 * HQ * 16


def block_kernel(nc, x, wq, wk, wv, wo, we, wr, wkf, wvf, mu, out):
    ctx = ExitStack()
    with ctx:
        def sb(name, shape, dt=F32):
            return ctx.enter_context(nc.sbuf_tensor(name, shape, dt))

        def ps(name, shape):
            return ctx.enter_context(nc.psum_tensor(name, shape, F32))

        def sem(name):
            return ctx.enter_context(nc.semaphore(name))

        def raw(ap):
            return ap.bitcast(F32)

        QS = sb("q_operands", [P, H, S], F32R)
        KS = sb("k_operands", [P, H, S], F32R)
        CAQ = sb("context_q_operands", [P, 2, S], F32R)
        CAK = sb("context_k_operands", [P, 2, S], F32R)
        CTX = sb("context_staged", [P, S], F32R)
        PT = sb("probabilities", [P, 2, HQ, S])
        XT = sb("x_tokens", [P, TT, D])
        ACC = sb("sum_tokens", [P, TT, D])
        XN = sb("xn_tokens", [P, TT, D])
        KACT = XN[:, :, :].rearrange("p t d -> p (t d)").rearrange("p (c s) -> p c s", c=CT)
        XNT = sb("xn_channels", [P, CT, 1 + S])
        XNH = sb("xn_high", [P, CT, S], F32R)
        XNL = sb("xn_low", [P, CT, S], F32R)
        MIX = sb("mixed", [P, CT, S])
        MIXH = sb("mixed_high", [P, CT, S], F32R)
        MIXL = sb("mixed_low", [P, CT, S], F32R)
        LATEH = sb("kact_or_attn_high", [P, CT, S], F32R)
        LATEL = sb("kact_or_attn_low", [P, CT, S], F32R)
        QH = sb("q_high", [P, CT, S], F32R)
        QL = sb("q_low", [P, CT, S], F32R)
        KH = sb("k_high", [P, CT, S], F32R)
        KL = sb("k_low", [P, CT, S], F32R)
        VP = sb("values_and_ones", [P, TT, H, 2 * DK])
        OS = sb("attn_quarter", [P, 2, S])
        OT = sb("attn_channels", [P, CT, S])
        DEN = sb("attn_denominators", [P, CT, S])
        R = sb("gate", [P, TT, D])
        NEGM = sb("negated_maxima", [PIECES, P], F32R)
        MX = sb("maxima", [P, PIECES])
        IDENT = sb("identity", [P, P])
        STATS = sb("ln_stats", [P, TT, 6])
        MV = sb("ln_mean_var", [P, TT, 2])
        EPSV = sb("ln_eps", [P, TT])
        HALF = sb("ln_minus_half", [P, TT])
        VE = sb("ln_var_eps", [P, TT])
        RSTD = sb("ln_rstd", [P, TT])
        MU = sb("mu", [P, 2, CT])
        OMM = sb("one_minus_mu", [P, 2, CT])
        names = ["we", "wq", "wk", "wkf", "wr", "wvf", "wv", "wo"]
        width = {w: D for w in names} | {"we": P}
        WH = {w: sb(w + "_high", [P, CT, width[w]], F32R) for w in names}
        WL = {w: sb(w + "_low", [P, CT, width[w]], F32R) for w in names}
        w_dram = dict(wq=wq, wk=wk, wv=wv, wo=wo, wr=wr, wkf=wkf, wvf=wvf, we=we)
        flat = PT[:, :, :, :].rearrange("p a h s -> p (a h s)")
        WRAW, at = {}, 0
        for w in names:
            WRAW[w] = flat[:, at:at + CT * width[w]].rearrange("p (c n) -> p c n", c=CT)
            at += CT * width[w]

        MAXB = ps("scores_for_max", [P, 2, S])
        ST = [ps(f"scores_{i}", [P, 2, S]) for i in range(2)]
        PV = ps("attn_sums", [P, S])
        JOB = ps("job_sums", [P, S])
        JOB2 = JOB[:, :].rearrange("p (i d) -> p i d", i=2)

        w_loaded = {w: sem(w + "_loaded") for w in names}
        mu_loaded = sem("mu_loaded")
        w_high = sem("w_high")
        w_split = sem("w_split")
        mu_ready = sem("mu_ready")
        zeroed = sem("zeroed")
        ident_zero = sem("ident_zero")
        ident_ready = sem("ident_ready")
        x_loaded = sem("x_loaded")
        stats_ready = sem("stats_ready")
        mv_ready = sem("mv_ready")
        var_ready = sem("var_ready")
        rstd_ready = sem("rstd_ready")
        xn_ready = sem("xn_ready")
        t_filled = sem("t_filled")
        xnt_ready = sem("xnt_ready")
        xn_high = sem("xn_high_ready")
        xn_split = sem("xn_split")
        qk_filled = sem("qk_filled")
        qk_high = sem("qk_high")
        qk_split = sem("qk_split")
        mix_scaled = sem("mix_scaled")
        mix_ready = sem("mix_ready")
        mix_high = sem("mix_high")
        mix_split = sem("mix_split")
        kf_filled = sem("kf_filled")
        relu_ready = sem("relu_ready")
        kact_ready = sem("kact_ready")
        kact_high = sem("kact_high")
        kact_split = sem("kact_split")
        ctx_filled = sem("ctx_filled")
        ctx_high = sem("ctx_high")
        ctx_staged = sem("ctx_staged")
        r_filled = sem("r_filled")
        r_ready = sem("r_ready")
        vf_filled = sem("vf_filled")
        vf_taken = sem("vf_taken")
        acc_loaded = sem("acc_loaded")
        acc_ready = sem("acc_ready")
        v_filled = sem("v_filled")
        v_ready = sem("v_ready")
        heads_loaded = [sem(f"heads_loaded{g}") for g in range(NQ)]
        ctx_rows_loaded = [sem(f"context_rows_loaded{g}") for g in range(NQ)]
        ca_loaded = [sem(f"context_loaded{g}") for g in range(2)]
        max_filled = sem("max_filled")
        max_taken = sem("max_taken")
        shift_loaded = sem("shift_loaded")
        st_filled = [sem(f"scores_filled{i}") for i in range(2)]
        exp_done = [sem(f"exp_done{i}") for i in range(2)]
        pv_done = sem("pv_done")
        o_taken = sem("o_taken")
        o_loaded = [sem(f"o_loaded{i}") for i in range(2)]
        den_ready = sem("den_ready")
        o_normed = sem("o_normed")
        o_high = sem("o_high")
        o_split = sem("o_split")
        wo_filled = sem("wo_filled")
        out_ready = sem("out_ready")
        stored = sem("stored")

        block = ctx.enter_context(nc.Block())

        def run(eng, body):
            body(0, False, True, True)
            with eng.Fori(1, B - 2) as b:
                body(b, True, True, True)
            body(B - 2, True, True, False)
            body(B - 1, True, False, False)

        def maxima_ahead(b, u):
            g, kt = divmod(u, TT)
            q = g + 1 if kt < TT - 1 else g + 2
            first = HQ * ((kt + 1) % TT)
            return q // NQ, q % NQ, range(first, first + HQ)

        @block.sync
        def _(sp):
            wait_values = [sp.alloc_register(f"wait_value{i}") for i in range(3)]

            def waits(*all_of):
                values = []
                for (_, v), r in zip(all_of, wait_values):
                    if not isinstance(v, int):
                        sp.reg_mov(r, v)
                        v = sp.snap(r)
                    values.append(v)
                for (s, _), v in zip(all_of, values):
                    sp.wait_ge(s, v)

            def load_x(n):
                waits((xn_ready, n))
                sp.dma_start(XT[:, :, :], x[bass.ds(n, 1)].rearrange("o (t p) d -> p (o t) d", p=P)
                             ).then_inc(x_loaded, 16)

            def load_acc(b):
                waits((stored, 16 * b))
                sp.dma_start(ACC[:, :, :], x[bass.ds(b, 1)].rearrange("o (t p) d -> p (o t) d", p=P)
                             ).then_inc(acc_loaded, 16)

            def load_head_rows(n, g):
                waits((qk_split, 4 * n + 2 * (g // 2) + 2))
                src = slice(64 * (g % 2), 64 * (g % 2) + 64)
                h4 = slice(HQ * g, HQ * g + HQ)
                for dst, row, t in ((QS, ROW_Q, QH), (QS, ROW_QK2, QH), (QS, ROW_LOW, QL),
                                    (KS, ROW_Q, KH), (KS, ROW_QK2, KL), (KS, ROW_LOW, KH)):
                    sp.dma_start(raw(dst[row:row + DK, h4, :]),
                                 raw(t[src, g // 2, :])).then_inc(heads_loaded[g], 16)

            def load_context_rows(n, g):
                waits((ctx_staged, n + 1))
                h4 = slice(HQ * g, HQ * g + HQ)
                for dst, r0 in ((QS, 0), (KS, 3 * DE)):
                    src = raw(CTX[r0:r0 + DE, :]).rearrange("p (o s) -> p o s", o=1)
                    sp.dma_start(raw(dst[0:DE, h4, :]),
                                 src.broadcast_to([DE, HQ, S])).then_inc(ctx_rows_loaded[g], 16)

            def load_context_operands(n, i):
                waits((ctx_staged, n + 1))
                sp.dma_start(raw(CAQ[0:2 * DE, i, :]), raw(CTX[0:2 * DE, :])).then_inc(ca_loaded[i], 16)
                sp.dma_start(raw(CAK[0:2 * DE, i, :]), raw(CTX[2 * DE:P, :])).then_inc(ca_loaded[i], 16)

            def load_shift(q, g):
                waits((max_taken, BANK_USES * (q + 1)))
                sp.dma_start(raw(QS[ROW_SHIFT:ROW_SHIFT + 1, HQ * g:HQ * g + HQ, :]),
                             raw(NEGM[:, :])).then_inc(shift_loaded, 16)

            def load_attn(b, g, has_prev=True):
                if has_prev:
                    waits((o_taken, 4 * b + g + 1), (o_split, 2 * b - 1 + g // 2))
                else:
                    waits((o_taken, 4 * b + g + 1))
                for j in range(HQ):
                    dst = slice(64 * (g % 2) + DK * j, 64 * (g % 2) + DK * j + DK)
                    for t, r0 in ((OT, 0), (DEN, DK)):
                        sp.dma_start(t[dst, g // 2, :], OS[32 * j + r0:32 * j + r0 + DK, g % 2, :]
                                     ).then_inc(o_loaded[g // 2], 16)

            def store(b):
                sp.dma_start(out[bass.ds(b, 1)].rearrange("o (t p) d -> p (o t) d", p=P), ACC[:, :, :]
                             ).then_inc(stored, 16)

            def scores_done(units):
                waits((st_filled[1], units))

            sp.dma_start(XT[:, :, :], x[0].rearrange("(t p) d -> p t d", p=P)).then_inc(x_loaded, 16)
            for w in names:
                src = w_dram[w].rearrange("(c p) n -> p c n", p=P)
                if w == "we":
                    for r in range(4):
                        sp.dma_start(WRAW[w][:, :, DE * r:DE * r + DE], src).then_inc(w_loaded[w], 16)
                    sp.dma_start(MU[:, :, :], mu).then_inc(mu_loaded, 16)
                else:
                    sp.dma_start(WRAW[w], src).then_inc(w_loaded[w], 16)
            sp.wait_ge(xn_ready, 1)
            sp.dma_start(XT[:, :, :], x[1].rearrange("(t p) d -> p t d", p=P)).then_inc(x_loaded, 16)
            load_context_operands(0, 0)
            for g in range(3):
                load_context_rows(0, g)
            sp.wait_ge(zeroed, 2)
            for g in range(3):
                load_head_rows(0, g)
            load_shift(0, 0)

            def body(b, has_prev, has_next, has_after):
                n = b + 1
                if has_prev:
                    scores_done(16 * b)
                load_context_operands(b, 1)
                load_context_rows(b, 3)
                if has_prev:
                    load_attn(b - 1, 3)
                load_head_rows(b, 3)
                load_shift(4 * b + 1, 1)
                scores_done(16 * b + 4)
                if has_next:
                    load_context_rows(n, 0)
                    load_head_rows(n, 0)
                load_attn(b, 0, has_prev)
                load_shift(4 * b + 2, 2)
                if has_prev:
                    waits((out_ready, 2 * b))
                    store(b - 1)
                scores_done(16 * b + 8)
                if has_next:
                    load_context_operands(n, 0)
                    load_context_rows(n, 1)
                    load_head_rows(n, 1)
                load_acc(b)
                load_attn(b, 1, has_prev)
                if has_after:
                    load_x(n + 1)
                load_shift(4 * b + 3, 3)
                scores_done(16 * b + 12)
                if has_next:
                    load_context_rows(n, 2)
                    load_head_rows(n, 2)
                load_attn(b, 2, has_prev)
                if has_next:
                    load_shift(4 * b + 4, 0)

            run(sp, body)
            load_attn(B - 1, 3)
            sp.wait_ge(out_ready, 2 * B)
            store(B - 1)
            sp.wait_ge(stored, 16 * B)

        @block.tensor
        def _(pe):
            mm = nc.tensor.matmul

            def product(dst, lhs, rhs):
                (lh, ll), (rh, rl) = lhs, rhs
                terms = [(a, c, k) for a, c in ((lh, rl), (ll, rh), (lh, rh)) for k in range(CT)]
                for i, (a, c, k) in enumerate(terms):
                    last = mm(dst, a(k), c(k), start=(i == 0), stop=(i == len(terms) - 1))
                return last

            def pair(high, low, cols):
                return (lambda k: high[:, k, cols]), (lambda k: low[:, k, cols])

            def cols(i, n=P):
                return slice(i * n, i * n + n)

            every = slice(None)

            def job_transpose(n, j):
                pe.wait_ge(xn_ready, n + 1)
                if j == 0:
                    pe.wait_ge(v_ready, 2 * n)
                else:
                    pe.wait_ge(xnt_ready, 2 * n + 1)
                for t in range(TT):
                    last = nc.tensor.transpose(JOB[:, cols(t)], XN[:, t, cols(j)], IDENT[:, :])
                last.then_inc(t_filled, 1)

            def weight(w):
                pe.wait_ge(w_split, names.index(w) + 1)

            def job_context(n):
                pe.wait_ge(xnt_ready, 2 * n + 2)
                pe.wait_ge(xn_split, n + 1)
                product(JOB[:, :], pair(WH["we"], WL["we"], every), pair(XNH, XNL, every)
                        ).then_inc(ctx_filled, 1)

            def job_qk(n, i, out_of=None):
                if i == 0:
                    pe.wait_ge(ctx_staged, n + 1)
                elif i == 2:
                    pe.wait_ge(relu_ready, 2 * n + 2)
                else:
                    pe.wait_ge(qk_split, 4 * n + i)
                w = ("wq", "wk")[i % 2]
                product(JOB[:, :], pair(WH[w], WL[w], cols(i // 2)), pair(XNH, XNL, every)
                        ).then_inc(qk_filled, 1)

            def job_kf(n, j, after_out=None):
                if j == 0:
                    pe.wait_ge(qk_split, 4 * n + 2)
                    pe.wait_ge(mix_split, 2 * n + 1)
                elif after_out is not None:
                    pe.wait_ge(out_ready, 2 * after_out + 2)
                else:
                    pe.wait_ge(relu_ready, 2 * n + 1)
                product(JOB[:, :], pair(WH["wkf"], WL["wkf"], cols(j)), pair(MIXH, MIXL, every)
                        ).then_inc(kf_filled, 1)

            def token_job(j, lhs, w, filled):
                for i in range(2):
                    last = product(JOB2[:, i, :], pair(*lhs, cols(2 * j + i)), pair(WH[w], WL[w], every))
                last.then_inc(filled, 1)

            def job_out(b, j, after_kf=None):
                if j == 0:
                    pe.wait_ge(o_split, 2 * b + 2)
                    if after_kf is not None:
                        pe.wait_ge(relu_ready, 2 * after_kf + 1)
                else:
                    pe.wait_ge(out_ready, 2 * b + 1)
                token_job(j, (LATEH, LATEL), "wo", wo_filled)

            def job_gate(n, j):
                if j == 0:
                    pe.wait_ge(qk_split, 4 * n + 4)
                    pe.wait_ge(mix_split, 2 * n + 2)
                else:
                    pe.wait_ge(r_ready, 2 * n + 1)
                token_job(j, (MIXH, MIXL), "wr", r_filled)

            def job_vf(n, j):
                if j == 0:
                    pe.wait_ge(r_ready, 2 * n + 2)
                    pe.wait_ge(kact_split, n + 1)
                else:
                    pe.wait_ge(vf_taken, 2 * n + 1)
                token_job(j, (LATEH, LATEL), "wvf", vf_filled)

            def job_v(n, j):
                if j == 0:
                    pe.wait_ge(vf_taken, 2 * n + 2)
                else:
                    pe.wait_ge(v_ready, 2 * n + 1)
                token_job(j, (XNH, XNL), "wv", v_filled)

            def max_piece(b, g, i):
                use = BANK_USES * (4 * b + g) + i
                if i == 0:
                    pe.wait_ge(ctx_rows_loaded[g], CA_DMAS * (b + 1))
                    pe.wait_ge(heads_loaded[g], HEAD_DMAS * (b + 1))
                if not isinstance(use, int) or use >= 2:
                    pe.wait_ge(max_taken, use - 1)
                h = HQ * g + i // TT
                mm(MAXB[:, (g + i) % 2, :], QS[0:ROW_QK2, h, cols(i % TT)], KS[0:ROW_QK2, h, :],
                   start=True, stop=True).then_inc(max_filled, 1)

            def shift_rows(b, g):
                pe.wait_ge(max_taken, BANK_USES * (4 * b + g) + PIECES)
                nc.tensor.transpose(MAXB[0:PIECES, (g + PIECES) % 2, 0:P], MX[:, :], IDENT[:, :]
                                    ).then_inc(max_filled, 1)

            def exact_scores(b, g, kt, half):
                u = 16 * b + 4 * g + kt
                if kt == 0 and half == 0:
                    pe.wait_ge(ca_loaded[g // 2], CA_DMAS * (b + 1))
                    pe.wait_ge(shift_loaded, 16 * (4 * b + g + 1))
                pe.wait_ge(exp_done[half], u)
                for j in range(2):
                    h = HQ * g + 2 * half + j
                    mm(ST[half][:, j, :], CAK[:, g // 2, cols(kt)], CAQ[:, g // 2, :],
                       start=True, stop=False)
                    last = mm(ST[half][:, j, :], KS[0:ROWS, h, cols(kt)], QS[0:ROWS, h, :],
                              start=False, stop=True)
                last.then_inc(st_filled[half], 1)

            def values(b, g, kt):
                u = 16 * b + 4 * g + kt
                if g == 0 and kt % 2 == 0:
                    pe.wait_ge(v_ready, 2 * b + kt // 2 + 1)
                if kt == 0:
                    pe.wait_ge(o_taken, 4 * b + g)
                for half in range(2):
                    pe.wait_ge(exp_done[half], u + 1)
                for j in range(HQ):
                    last = mm(PV[32 * j:32 * j + 32, :], VP[:, kt, HQ * g + j, :], PT[:, u_par(kt), j, :],
                              start=(kt == 0), stop=(kt == TT - 1))
                last.then_inc(pv_done, 1)

            def u_par(kt):
                return kt % 2

            pe.wait_ge(ident_ready, 1)
            for j in range(CT):
                job_transpose(0, j)
            weight("we")
            job_context(0)
            weight("wq")
            job_qk(0, 0)
            weight("wk")
            job_qk(0, 1)
            weight("wkf")
            for j in range(CT):
                job_kf(0, j)
            for i in range(2, 4):
                job_qk(0, i)
            weight("wr")
            for j in range(2):
                job_gate(0, j)
            weight("wvf")
            for j in range(2):
                job_vf(0, j)
            weight("wv")
            for j in range(2):
                job_v(0, j)
            for i in range(PIECES):
                max_piece(0, 0, i)
            shift_rows(0, 0)
            for i in range(HQ):
                max_piece(0, 1, i)
            weight("wo")
            pe.wait_ge(zeroed, 4)

            def body(b, has_prev, has_next, has_after):
                n = b + 1

                def first_job(u):
                    if has_next:
                        if u == 1:
                            job_transpose(n, 0)
                        if u == 3:
                            job_context(n)
                        if u == 4:
                            job_qk(n, 1)
                        if u == 5:
                            job_kf(n, 0)
                    if has_prev and 6 <= u < 8:
                        if u == 6 and not has_next:
                            pe.wait_ge(v_ready, 2 * b + 2)
                        job_out(b - 1, u - 6, n if has_next else None)
                    if has_next:
                        if u == 8:
                            job_kf(n, 1, b - 1 if has_prev else None)
                        if 9 <= u < 11:
                            job_qk(n, u - 7)
                        if u == 11:
                            job_gate(n, 0)
                        if 12 <= u < 14:
                            job_vf(n, u - 12)
                        if u >= 14:
                            job_v(n, u - 14)

                def second_job(u):
                    if has_next:
                        if u == 1:
                            job_transpose(n, 1)
                        if u == 3:
                            job_qk(n, 0)
                        if u == 11:
                            job_gate(n, 1)

                for u in range(NU):
                    g, kt = divmod(u, TT)
                    later, q, pieces = maxima_ahead(b, u)
                    look = not later or has_next
                    if kt == TT - 1 and (g < NQ - 1 or has_next):
                        shift_rows(b + (g + 1) // NQ, (g + 1) % NQ)
                    if look:
                        max_piece(b + later, q, pieces[0])
                    exact_scores(b, g, kt, 0)
                    if look:
                        max_piece(b + later, q, pieces[1])
                    first_job(u)
                    exact_scores(b, g, kt, 1)
                    if look:
                        max_piece(b + later, q, pieces[2])
                    second_job(u)
                    if look:
                        max_piece(b + later, q, pieces[3])
                    if u > 0:
                        values(b, (u - 1) // TT, (u - 1) % TT)
                    elif has_prev:
                        values(b - 1, NQ - 1, TT - 1)

            run(pe, body)
            values(B - 1, NQ - 1, TT - 1)
            for j in range(2):
                job_out(B - 1, j)

        @block.scalar
        def _(act):
            A = nc.scalar.activation

            def exps(b, g, kt, half):
                u = 16 * b + 4 * g + kt
                if half == 0 and (not isinstance(u, int) or u > 1):
                    act.wait_ge(pv_done, u - 1)
                act.wait_ge(st_filled[half], u + 1)
                A(PT[:, kt % 2, 2 * half:2 * half + 2, :], ST[half][:, :, :], ACT.Exp
                  ).then_inc(exp_done[half], 1)

            def take_attn(b, g):
                act.wait_ge(pv_done, 16 * b + 4 * (g + 1))
                if g >= 2:
                    act.wait_ge(o_loaded[0], O_DMAS * (2 * b + 2))
                else:
                    act.wait_ge(o_loaded[1], O_DMAS * (2 * b))
                A(OS[:, g % 2, :], PV[:, :], ACT.Copy).then_inc(o_taken, 1)

            def take_transpose(n, j):
                if j == 0:
                    act.wait_ge(mix_split, 2 * n)
                    act.wait_ge(xn_split, n)
                act.wait_ge(t_filled, 2 * n + j + 1)
                A(XNT[:, j, 1:], JOB[:, :], ACT.Copy).then_inc(xnt_ready, 1)

            def scale_before(n, i):
                act.wait_ge(xnt_ready, 2 * n + 2)
                act.wait_ge(mix_split, 2 * n + i)
                for c in range(CT):
                    A(MIX[:, c, :], XNT[:, c, 0:S], ACT.Copy, scale=OMM[:, i, c:c + 1]
                      ).then_inc(mix_scaled, 1)

            def qk_highs(n, i):
                act.wait_ge(qk_filled, 4 * n + i + 1)
                if i % 2 == 0:
                    for g in (i, i + 1):
                        act.wait_ge(heads_loaded[g], HEAD_DMAS * n)
                A((QH, KH)[i % 2][:, i // 2, :], JOB[:, :], ACT.Copy, scale=(SCALE, 1.0)[i % 2]
                  ).then_inc(qk_high, 1)

            def relus(n, j):
                act.wait_ge(kf_filled, 2 * n + j + 1)
                act.wait_ge(t_filled, 2 * n + 2)
                A(KACT[:, j, :], JOB[:, :], ACT.Relu).then_inc(relu_ready, 1)

            def context_highs(n):
                act.wait_ge(ctx_filled, n + 1)
                for g in range(NQ):
                    act.wait_ge(ctx_rows_loaded[g], CA_DMAS * n)
                for i in range(2):
                    act.wait_ge(ca_loaded[i], CA_DMAS * n)
                A(CTX[0:2 * DE, :], JOB[0:2 * DE, :], ACT.Copy)
                A(CTX[2 * DE:P, :], JOB[2 * DE:P, :], ACT.Copy, scale=INFLUENCE).then_inc(ctx_high, 1)

            def gates(n, j):
                act.wait_ge(r_filled, 2 * n + j + 1)
                act.wait_ge(acc_ready, 2 * n)
                A(R[:, 2 * j:2 * j + 2, :], JOB2[:, :, :], ACT.Sigmoid).then_inc(r_ready, 1)

            def take_values(n, j, has_prev=True):
                act.wait_ge(v_filled, 2 * n + j + 1)
                if has_prev:
                    act.wait_ge(pv_done, 16 * n - 2 + 2 * j)
                A(VP[:, 2 * j:2 * j + 2, :, 0:DK],
                  JOB2[:, :, :].rearrange("p i (h d) -> p i h d", h=H), ACT.Copy).then_inc(v_ready, 1)

            for i, w in enumerate(names):
                act.wait_ge(w_loaded[w], 16 * (4 if w == "we" else 1))
                A(WH[w][:, :, :], WRAW[w], ACT.Copy).then_inc(w_high, 1)
                if i == 1:
                    act.wait_ge(zeroed, 6)
                    for j in range(CT):
                        take_transpose(0, j)
            act.wait_ge(mu_ready, 1)
            context_highs(0)
            for i in range(2):
                qk_highs(0, i)
            scale_before(0, 0)
            for j in range(2):
                relus(0, j)
            for i in range(2, 4):
                qk_highs(0, i)
            scale_before(0, 1)
            for j in range(2):
                gates(0, j)
            for j in range(2):
                take_values(0, j, False)

            def body(b, has_prev, has_next, has_after):
                n = b + 1

                def after_first(u):
                    if has_next:
                        if u == 1:
                            take_transpose(n, 0)
                        if u == 3:
                            context_highs(n)
                        if u == 4:
                            qk_highs(n, 1)
                        if u == 5:
                            relus(n, 0)
                        if u == 8:
                            relus(n, 1)
                        if 9 <= u < 11:
                            qk_highs(n, u - 7)

                def after_second(u):
                    if has_prev and u == 0:
                        take_values(b, 1)
                    if has_next:
                        if u == 1:
                            take_transpose(n, 1)
                        if u == 2:
                            scale_before(n, 0)
                        if u == 3:
                            qk_highs(n, 0)
                        if u == 7:
                            scale_before(n, 1)
                        if u == 11:
                            for j in range(2):
                                gates(n, j)
                        if u == 14:
                            take_values(n, 0)

                for u in range(NU):
                    g, kt = divmod(u, TT)
                    exps(b, g, kt, 0)
                    after_first(u)
                    exps(b, g, kt, 1)
                    after_second(u)
                    if kt == 0 and g > 0:
                        take_attn(b, g - 1)
                    elif u == 0 and has_prev:
                        take_attn(b - 1, NQ - 1)

            run(act, body)
            take_attn(B - 1, NQ - 1)

        @block.vector
        def _(dve):
            V = nc.vector

            def row_maximum(b, g, i):
                dve.wait_ge(max_filled, BANK_USES * (4 * b + g) + i + 1)
                V.reduce_max(MX[:, i:i + 1], MAXB[:, (g + i) % 2, :], AX.X).then_inc(max_taken, 1)

            def take_shift(b, g):
                q = 4 * b + g
                dve.wait_ge(max_filled, BANK_USES * (q + 1))
                dve.wait_ge(shift_loaded, 16 * q)
                V.tensor_scalar(NEGM[:, :], MAXB[0:PIECES, (g + PIECES) % 2, 0:P], -1.0, None, ALU.mult
                                ).then_inc(max_taken, 1)

            def layernorm_stats(n):
                dve.wait_ge(x_loaded, 16 * (n + 1))
                for t in range(TT):
                    last = V.bn_stats(STATS[:, t, :], XT[:, t, :])
                last.then_inc(stats_ready, 1)

            def layernorm_moments(n):
                for t in range(TT):
                    last = V.bn_aggr(MV[:, t, :], STATS[:, t, :])
                last.then_inc(mv_ready, 1)

            def layernorm(n):
                dve.wait_ge(rstd_ready, n + 1)
                dve.wait_ge(kact_split, n)
                for t in range(TT):
                    last = V.tensor_scalar(XN[:, t, :], XT[:, t, :], MV[:, t, 0:1], RSTD[:, t:t + 1],
                                           ALU.subtract, ALU.mult)
                last.then_inc(xn_ready, 1)

            def xn_highs(n):
                dve.wait_ge(xnt_ready, 2 * n + 2)
                dve.wait_ge(v_filled, 2 * n)
                V.tensor_copy(XNH[:, :, :], XNT[:, :, 1:]).then_inc(xn_high, 1)

            def qk_lows(n, i):
                dve.wait_ge(qk_high, 4 * n + i + 1)
                high, low = ((QH, QL), (KH, KL))[i % 2]
                V.scalar_tensor_tensor(out=low[:, i // 2, :], in0=JOB[:, :], scalar=(SCALE, 1.0)[i % 2],
                                       in1=raw(high[:, i // 2, :]), op0=ALU.mult, op1=ALU.subtract
                                       ).then_inc(qk_split, 1)

            def mix(n, i):
                for c in range(CT):
                    dve.wait_ge(mix_scaled, 4 * n + 2 * i + c + 1)
                    last = V.scalar_tensor_tensor(out=MIX[:, c, :], in0=XNT[:, c, 1:], scalar=MU[:, i, c:c + 1],
                                                  in1=MIX[:, c, :], op0=ALU.mult, op1=ALU.add)
                last.then_inc(mix_ready, 1)
                dve.wait_ge(mix_ready, 2 * n + i + 1)
                if i == 0:
                    dve.wait_ge(r_filled, 2 * n)
                else:
                    dve.wait_ge(kf_filled, 2 * n + 2)
                V.tensor_copy(MIXH[:, :, :], MIX[:, :, :]).then_inc(mix_high, 1)

            def kact_highs(n, b=None):
                dve.wait_ge(kact_ready, 2 * n + 2)
                if b is not None:
                    dve.wait_ge(wo_filled, 2 * b)
                V.tensor_copy(LATEH[:, :, :], KACT).then_inc(kact_high, 1)

            def context_lows(n):
                dve.wait_ge(ctx_high, n + 1)
                V.tensor_tensor(CTX[DE:2 * DE, :], JOB[DE:2 * DE, :], raw(CTX[DE:2 * DE, :]), ALU.subtract)
                V.scalar_tensor_tensor(out=CTX[2 * DE:3 * DE, :], in0=JOB[2 * DE:3 * DE, :], scalar=INFLUENCE,
                                       in1=raw(CTX[2 * DE:3 * DE, :]), op0=ALU.mult, op1=ALU.subtract
                                       ).then_inc(ctx_staged, 1)

            def take_vf(n, j):
                r = R[:, 2 * j:2 * j + 2, :]
                dve.wait_ge(vf_filled, 2 * n + j + 1)
                dve.wait_ge(r_ready, 2 * n + j + 1)
                V.tensor_tensor(r, JOB2[:, :, :], r, ALU.mult).then_inc(vf_taken, 1)

            def invert_sums(b, t, i):
                if i == 0:
                    dve.wait_ge(o_loaded[t], O_DMAS * 2 * (b + 1))
                V.reciprocal(DEN[:, t, i * P:i * P + P], DEN[:, t, i * P:i * P + P]).then_inc(den_ready, 1)

            def norm_attn(b, t):
                dve.wait_ge(den_ready, TT * (2 * b + t + 1))
                V.tensor_tensor(OT[:, t, :], OT[:, t, :], DEN[:, t, :], ALU.mult).then_inc(o_normed, 1)

            def attn_highs(b, t, n=None):
                dve.wait_ge(o_normed, 2 * b + t + 1)
                if n is not None:
                    dve.wait_ge(vf_filled, 2 * n + 2)
                elif t == 0:
                    dve.wait_ge(wo_filled, 2 * b)
                V.tensor_copy(LATEH[:, t, :], OT[:, t, :]).then_inc(o_high, 1)

            def take_out(b, j):
                acc = ACC[:, 2 * j:2 * j + 2, :]
                dve.wait_ge(wo_filled, 2 * b + j + 1)
                dve.wait_ge(acc_ready, 2 * b + 2)
                V.tensor_tensor(acc, JOB2[:, :, :], acc, ALU.add).then_inc(out_ready, 1)

            layernorm_stats(0)
            V.memset(raw(QS[64:P, :, :]), 0.0).then_inc(zeroed, 1)
            V.memset(raw(KS[64:P, :, :]), 1.0).then_inc(zeroed, 1)
            V.memset(raw(CAQ[2 * DE:P, :, :]), 0.0).then_inc(zeroed, 1)
            V.memset(raw(CAK[2 * DE:P, :, :]), 0.0).then_inc(zeroed, 1)
            V.memset(XNT[:, :, 0:1], 0.0).then_inc(zeroed, 1)
            V.memset(VP[:, :, :, :], 1.0).then_inc(zeroed, 1)
            dve.wait_ge(stats_ready, 1)
            layernorm_moments(0)
            layernorm(0)

            def weight_low(i):
                w = names[i]
                dve.wait_ge(w_high, i + 1)
                V.tensor_tensor(WL[w][:, :, :], WRAW[w], raw(WH[w][:, :, :]), ALU.subtract
                                ).then_inc(w_split, 1)

            dve.wait_ge(mu_loaded, 16)
            V.tensor_scalar(OMM[:, :, :], MU[:, :, :], -1.0, 1.0, ALU.mult, ALU.add).then_inc(mu_ready, 1)
            for i in range(2):
                weight_low(i)
            xn_highs(0)
            for i in range(2, len(names)):
                weight_low(i)
            context_lows(0)
            for i in range(2):
                qk_lows(0, i)
            mix(0, 0)
            for i in range(2, 4):
                qk_lows(0, i)
            kact_highs(0)
            mix(0, 1)
            for j in range(2):
                take_vf(0, j)
            layernorm_stats(1)
            for i in range(PIECES):
                row_maximum(0, 0, i)
            take_shift(0, 0)
            dve.wait_ge(stats_ready, 2)
            layernorm_moments(1)
            for i in range(HQ):
                row_maximum(0, 1, i)
            layernorm(1)

            def body(b, has_prev, has_next, has_after):
                n = b + 1

                def after_first(u):
                    if has_next:
                        if u == 2:
                            xn_highs(n)
                        if u == 3:
                            context_lows(n)

                def after_second(u):
                    if has_next:
                        if u == 4:
                            qk_lows(n, 1)
                        if 9 <= u < 11:
                            qk_lows(n, u - 7)
                        if 12 <= u < 14:
                            take_vf(n, u - 12)
                    if has_prev and 6 <= u < 8:
                        take_out(b - 1, u - 6)

                def at_end(u):
                    if has_prev:
                        if 3 <= u < 5:
                            for i in range(2):
                                invert_sums(b - 1, 1, 2 * (u - 3) + i)
                        if u == 5:
                            norm_attn(b - 1, 1)
                            attn_highs(b - 1, 1)
                    if has_next:
                        if u == 3:
                            mix(n, 0)
                        if u == 9:
                            mix(n, 1)
                        if u == 10:
                            kact_highs(n, b if has_prev else None)
                    if 11 <= u < 13:
                        for i in range(2):
                            invert_sums(b, 0, 2 * (u - 11) + i)
                    if u == 13:
                        norm_attn(b, 0)
                        attn_highs(b, 0, n if has_next else None)
                    if has_after:
                        if u == 12:
                            layernorm_stats(n + 1)
                        if u == 13:
                            layernorm_moments(n + 1)
                        if u == 15:
                            layernorm(n + 1)

                for u in range(NU):
                    g, kt = divmod(u, TT)
                    later, q, pieces = maxima_ahead(b, u)
                    look = not later or has_next
                    if kt == TT - 1 and (g < NQ - 1 or has_next):
                        take_shift(b + (g + 1) // NQ, (g + 1) % NQ)
                    if has_next and u == 4:
                        qk_lows(n, 0)
                    if u == 13 and has_after:
                        dve.wait_ge(stats_ready, n + 2)
                    if look:
                        row_maximum(b + later, q, pieces[0])
                        row_maximum(b + later, q, pieces[1])
                    after_first(u)
                    if look:
                        row_maximum(b + later, q, pieces[2])
                    after_second(u)
                    if look:
                        row_maximum(b + later, q, pieces[3])
                    at_end(u)

            run(dve, body)
            for i in range(TT):
                invert_sums(B - 1, 1, i)
            norm_attn(B - 1, 1)
            attn_highs(B - 1, 1)
            for j in range(2):
                take_out(B - 1, j)

        @block.gpsimd
        def _(pool):
            G = nc.gpsimd

            def rstd(n):
                pool.wait_ge(mv_ready, n + 1)
                pool.wait_ge(xn_ready, n)
                G.tensor_tensor(VE[:, :], MV[:, :, 1], EPSV[:, :], ALU.add).then_inc(var_ready, 1)
                pool.wait_ge(var_ready, n + 1)
                G.tensor_tensor(RSTD[:, :], VE[:, :], HALF[:, :], ALU.pow).then_inc(rstd_ready, 1)

            def lows(ready, count, low, whole, high, done):
                pool.wait_ge(ready, count)
                G.tensor_tensor(low, whole, raw(high), ALU.subtract).then_inc(done, 1)

            def xn_lows(n):
                lows(xn_high, n + 1, XNL[:, :, :], XNT[:, :, 1:], XNH[:, :, :], xn_split)

            def mix_lows(n, i):
                lows(mix_high, 2 * n + i + 1, MIXL[:, :, :], MIX[:, :, :], MIXH[:, :, :], mix_split)

            def kacts(n, c):
                pool.wait_ge(relu_ready, 2 * n + c + 1)
                G.tensor_tensor(KACT[:, c, :], KACT[:, c, :], KACT[:, c, :], ALU.mult
                                ).then_inc(kact_ready, 1)

            def kact_lows(n):
                lows(kact_high, n + 1, LATEL[:, :, :], KACT, LATEH[:, :, :], kact_split)

            def attn_lows(b, t):
                lows(o_high, 2 * b + t + 1, LATEL[:, t, :], OT[:, t, :], LATEH[:, t, :], o_split)

            def add_vf(n, j):
                pool.wait_ge(vf_taken, 2 * n + j + 1)
                pool.wait_ge(acc_loaded, 16 * (n + 1))
                acc = ACC[:, 2 * j:2 * j + 2, :]
                G.tensor_tensor(acc, acc, R[:, 2 * j:2 * j + 2, :], ALU.add).then_inc(acc_ready, 1)

            G.memset(IDENT[:, :], 0.0).then_inc(ident_zero, 1)
            pool.wait_ge(ident_zero, 1)
            G.affine_select(out=IDENT[:, :], in_=IDENT[:, :], compare_op=ALU.not_equal, fill=1.0, base=0,
                            pattern=[[-1, P]], channel_multiplier=1).then_inc(ident_ready, 1)
            G.memset(EPSV[:, :], EPS).then_inc(ident_zero, 1)
            G.memset(HALF[:, :], -0.5).then_inc(ident_zero, 1)
            pool.wait_ge(ident_zero, 3)
            rstd(0)
            xn_lows(0)
            mix_lows(0, 0)
            for c in range(CT):
                kacts(0, c)
            mix_lows(0, 1)
            kact_lows(0)
            rstd(1)

            def body(b, has_prev, has_next, has_after):
                n = b + 1
                if has_next:
                    xn_lows(n)
                    mix_lows(n, 0)
                if has_prev:
                    attn_lows(b - 1, 1)
                if has_next:
                    for c in range(CT):
                        kacts(n, c)
                    mix_lows(n, 1)
                    kact_lows(n)
                for j in range(2):
                    add_vf(b, j)
                if has_after:
                    rstd(n + 1)
                attn_lows(b, 0)

            run(pool, body)
            attn_lows(B - 1, 1)


_INS = ["x", "wq", "wk", "wv", "wo", "we", "wr", "wkf", "wvf", "mu"]


def kernel(L0_attn_X, L0_attn_Wq, L0_attn_Wk, L0_attn_Wv, L0_attn_Wo, L0_attn_We,
           L0_ffn_W_r, L0_ffn_W_k, L0_ffn_W_v, L0_ffn_mu_r, L0_ffn_mu_k):
    import numpy as np
    import concourse.bacc as bacc
    from concourse.bass_utils import run_bass_kernel_spmd

    def by_channel(w):
        w = np.asarray(w).T.reshape(D, H // HQ, HQ, DK)
        return np.ascontiguousarray(w.transpose(0, 1, 3, 2).reshape(D, D))

    def turned(w):
        return np.ascontiguousarray(np.asarray(w).T)

    arrays = {
        "x": np.ascontiguousarray(L0_attn_X),
        "wq": by_channel(L0_attn_Wq), "wk": by_channel(L0_attn_Wk), "wv": turned(L0_attn_Wv),
        "wo": turned(L0_attn_Wo), "we": turned(L0_attn_We), "wr": turned(L0_ffn_W_r),
        "wkf": turned(L0_ffn_W_k), "wvf": turned(L0_ffn_W_v),
        "mu": np.ascontiguousarray(np.stack([L0_ffn_mu_k, L0_ffn_mu_r]).reshape(2, CT, P).transpose(2, 0, 1)),
    }
    nc = bacc.Bacc("TRN2", target_bir_lowering=False, num_devices=1)
    args = [nc.dram_tensor(f"in_{k}", arrays[k].shape, mybir.dt.from_np(arrays[k].dtype),
                           kind="ExternalInput").ap() for k in _INS]
    out = nc.dram_tensor("out_0", (B, S, D), F32, kind="ExternalOutput").ap()
    block_kernel(nc, *args, out)
    r = run_bass_kernel_spmd(nc, [{f"in_{k}": arrays[k] for k in _INS}], core_ids=[0])
    return r.results[0]["out_0"]
```

```python
from contextlib import ExitStack

import concourse.bass as bass
from concourse import mybir

F32 = mybir.dt.float32
F32R = mybir.dt.float32r
ALU = mybir.AluOpType
ACT = mybir.ActivationFunctionType
AX = mybir.AxisListType

P = 128
B, S, D = 8, 512, 256
H, DK, DE = 16, 16, 32
CT = D // P
TT = S // P
HQ = 4
NQ = H // HQ
NU = NQ * TT
PIECES = HQ * TT
WARM_UP = 22
TERMS = 3 * CT
BANK_USES = PIECES + 1
SCALE = float(DK) ** -0.5
INFLUENCE = 0.1
EPS = 1e-5
ROW_Q = 32
ROW_QK2 = ROW_Q + DK
ROW_LOW = ROW_QK2 + DK
ROW_SHIFT = ROW_LOW + DK
ROWS = 97
MAXIMA_DMAS = 2 * 16
HEAD_DMAS = 4 * 16
CTX_DMAS = 2 * 16
CA_DMAS = 4 * 16
O_DMAS = 16


def block_kernel(nc, x, wq, wk, wv, wo, we, wr, wkf, wvf, mu, out):
    ctx = ExitStack()
    with ctx:
        def sb(name, shape, dt=F32):
            return ctx.enter_context(nc.sbuf_tensor(name, shape, dt))

        def ps(name, shape):
            return ctx.enter_context(nc.psum_tensor(name, shape, F32))

        def sem(name):
            return ctx.enter_context(nc.semaphore(name))

        def raw(ap):
            return ap.bitcast(F32)

        QS = sb("q_operands", [P, H, S], F32R)
        KS = sb("k_operands", [P, H, S], F32R)
        CAQ = sb("context_q_operands", [P, 2, S], F32R)
        CAK = sb("context_k_operands", [P, 2, S], F32R)
        CTX = sb("context_staged", [P, S], F32R)
        PT = sb("probabilities", [P, 2, HQ, S])
        XT = sb("x_tokens", [P, TT, D])
        ACC = sb("sum_tokens", [P, TT, D])
        XN = sb("xn_tokens", [P, TT, D])
        KACT = XN[:, :, :].rearrange("p t d -> p (t d)").rearrange("p (c s) -> p c s", c=CT)
        XNT = sb("xn_channels", [P, CT, 1 + S])
        XNH = sb("xn_high", [P, CT, S], F32R)
        XNL = sb("xn_low", [P, CT, S], F32R)
        MIX = sb("mixed", [P, CT, S])
        MIXH = sb("mixed_high", [P, CT, S], F32R)
        MIXL = sb("mixed_low", [P, CT, S], F32R)
        LATEH = sb("kact_or_attn_high", [P, CT, S], F32R)
        LATEL = sb("kact_or_attn_low", [P, CT, S], F32R)
        QH = sb("q_high", [P, CT, S], F32R)
        QL = sb("q_low", [P, CT, S], F32R)
        KH = sb("k_high", [P, CT, S], F32R)
        KL = sb("k_low", [P, CT, S], F32R)
        VP = sb("values_and_ones", [P, TT, H, DK, 2])
        OS = sb("attn_quarter", [P, 2, S])
        OD = sb("attn_channels", [P, CT, 2, S])
        OT, DEN = OD[:, :, 0, :], OD[:, :, 1, :]
        R = sb("gate", [P, TT, D])
        NEGM = sb("negated_maxima", [PIECES, P], F32R)
        MX = sb("maxima", [P, PIECES])
        IDENT = sb("identity", [P, P])
        STATS = sb("ln_stats", [P, TT, 6])
        MV = sb("ln_mean_var", [P, TT, 2])
        EPSV = sb("ln_eps", [P, TT])
        HALF = sb("ln_minus_half", [P, TT])
        VE = sb("ln_var_eps", [P, TT])
        RSTD = sb("ln_rstd", [P, TT])
        MU = sb("mu", [P, 2, CT])
        OMM = sb("one_minus_mu", [P, 2, CT])
        FACTOR = sb("context_factor", [P, 1])
        names = ["we", "wq", "wk", "wv", "wkf", "wvf", "wr", "wo"]
        width = {w: D for w in names} | {"we": P}
        WH = {w: sb(w + "_high", [P, CT, width[w]], F32R) for w in names}
        WL = {w: sb(w + "_low", [P, CT, width[w]], F32R) for w in names}
        w_dram = dict(wq=wq, wk=wk, wv=wv, wo=wo, wr=wr, wkf=wkf, wvf=wvf, we=we)
        flat = PT[:, :, :, :].rearrange("p a h s -> p (a h s)")
        WRAW, at = {}, 0
        for w in names:
            WRAW[w] = flat[:, at:at + CT * width[w]].rearrange("p (c n) -> p c n", c=CT)
            at += CT * width[w]
        FILL = flat[:, at:at + P]

        MAXB = ps("scores_for_max", [P, 2, S])
        ST = [ps(f"scores_{i}", [P, 2, S]) for i in range(2)]
        PV = ps("attn_sums", [P, S])
        JOB = ps("job_sums", [P, S])
        FIRST = [JOB[:, :], PV[:, :], ST[0][:, 0, :], ST[0][:, 1, :], ST[1][:, 0, :], ST[1][:, 1, :]]

        def token_tiles(bank):
            return bank.rearrange("p (i d) -> p i d", i=2)

        w_loaded = {w: sem(w + "_loaded") for w in names}
        mu_loaded = sem("mu_loaded")
        w_halved = sem("w_halved")
        w_high = sem("w_high")
        w_split = sem("w_split")
        w_late_split = sem("w_late_split")
        mu_ready = sem("mu_ready")
        zeroed = sem("zeroed")
        ones_ready = sem("ones_ready")
        fill_ready = sem("fill_ready")
        filled_up = sem("filled_up")
        ident_zero = sem("ident_zero")
        ident_ready = sem("ident_ready")
        x_loaded = sem("x_loaded")
        stats_ready = sem("stats_ready")
        mv_ready = sem("mv_ready")
        var_ready = sem("var_ready")
        rstd_ready = sem("rstd_ready")
        xn_ready = sem("xn_ready")
        t_filled = sem("t_filled")
        xnt_ready = sem("xnt_ready")
        first_high = sem("first_high")
        xn_split = sem("xn_split")
        qk_filled = sem("qk_filled")
        qk_high = sem("qk_high")
        qk_split = sem("qk_split")
        mix_scaled = sem("mix_scaled")
        mix_ready = sem("mix_ready")
        mix_high = sem("mix_high")
        mix_split = sem("mix_split")
        kf_filled = sem("kf_filled")
        relu_ready = sem("relu_ready")
        kact_ready = sem("kact_ready")
        kact_high = sem("kact_high")
        kact_split = sem("kact_split")
        ctx_filled = sem("ctx_filled")
        ctx_high = sem("ctx_high")
        ctx_staged = sem("ctx_staged")
        r_filled = sem("r_filled")
        r_ready = sem("r_ready")
        vf_filled = sem("vf_filled")
        vf_taken = sem("vf_taken")
        acc_loaded = sem("acc_loaded")
        acc_ready = sem("acc_ready")
        v_filled = sem("v_filled")
        v_ready = sem("v_ready")
        maxima_rows_loaded = [sem(f"maxima_rows_loaded{g}") for g in range(NQ)]
        heads_loaded = [sem(f"heads_loaded{g}") for g in range(NQ)]
        ctx_rows_loaded = [sem(f"context_rows_loaded{g}") for g in range(NQ)]
        ca_loaded = [sem(f"context_loaded{g}") for g in range(2)]
        max_filled = sem("max_filled")
        max_taken = sem("max_taken")
        shift_loaded = sem("shift_loaded")
        st_filled = [sem(f"scores_filled{i}") for i in range(2)]
        exp_done = [sem(f"exp_done{i}") for i in range(2)]
        pv_done = sem("pv_done")
        o_taken = sem("o_taken")
        o_loaded = [sem(f"o_loaded{i}") for i in range(2)]
        den_ready = sem("den_ready")
        last_normed = sem("last_normed")
        last_high = sem("last_high")
        last_split = sem("last_split")
        o_normed = sem("o_normed")
        o_high = sem("o_high")
        o_split = sem("o_split")
        wo_filled = sem("wo_filled")
        out_ready = sem("out_ready")
        stored = sem("stored")

        block = ctx.enter_context(nc.Block())

        def run(eng, body):
            body(0, False, True, True)
            with eng.Fori(1, B - 2) as b:
                body(b, True, True, True)
            body(B - 2, True, True, False)
            body(B - 1, True, False, False)

        def maxima_ahead(b, u):
            g, kt = divmod(u, TT)
            q = g + 1 if kt < TT - 1 else g + 2
            first = HQ * ((kt + 1) % TT)
            return q // NQ, q % NQ, range(first, first + HQ)

        @block.sync
        def _(sp):
            wait_values = [sp.alloc_register(f"wait_value{i}") for i in range(3)]

            def waits(*all_of):
                values = []
                for (_, v), r in zip(all_of, wait_values):
                    if not isinstance(v, int):
                        sp.reg_mov(r, v)
                        v = sp.snap(r)
                    values.append(v)
                for (s, _), v in zip(all_of, values):
                    sp.wait_ge(s, v)

            def load_x(n):
                waits((xn_ready, n))
                sp.dma_start(XT[:, :, :], x[bass.ds(n, 1)].rearrange("o (t p) d -> p (o t) d", p=P)
                             ).then_inc(x_loaded, 16)

            def load_acc(b):
                waits((stored, 16 * b))
                sp.dma_start(ACC[:, :, :], x[bass.ds(b, 1)].rearrange("o (t p) d -> p (o t) d", p=P)
                             ).then_inc(acc_loaded, 16)

            def load_rows(n, g, rows, loaded):
                waits((qk_split, 4 * n + 2 * (g // 2) + 2))
                src = slice(64 * (g % 2), 64 * (g % 2) + 64)
                h4 = slice(HQ * g, HQ * g + HQ)
                for dst, row, t in rows:
                    sp.dma_start(raw(dst[row:row + DK, h4, :]), raw(t[src, g // 2, :])).then_inc(loaded[g], 16)

            def load_head_rows(n, g):
                load_rows(n, g, ((QS, ROW_Q, QH), (KS, ROW_Q, KH)), maxima_rows_loaded)
                load_rows(n, g, ((QS, ROW_QK2, QH), (QS, ROW_LOW, QL), (KS, ROW_QK2, KL),
                                 (KS, ROW_LOW, KH)), heads_loaded)

            def load_context_rows(n, g):
                waits((ctx_staged, n + 1))
                h4 = slice(HQ * g, HQ * g + HQ)
                for dst, r0 in ((QS, 0), (KS, DE)):
                    src = raw(CTX[r0:r0 + DE, :]).rearrange("p (o s) -> p o s", o=1)
                    sp.dma_start(raw(dst[0:DE, h4, :]),
                                 src.broadcast_to([DE, HQ, S])).then_inc(ctx_rows_loaded[g], 16)

            def load_context_operands(n, i):
                waits((ctx_staged, n + 1))
                for dst, row, r0 in ((CAQ, 0, 0), (CAK, 0, 3 * DE), (CAQ, DE, 2 * DE), (CAK, DE, DE)):
                    sp.dma_start(raw(dst[row:row + DE, i, :]), raw(CTX[r0:r0 + DE, :])
                                 ).then_inc(ca_loaded[i], 16)

            def load_shift(q, g):
                waits((max_taken, BANK_USES * (q + 1)))
                sp.dma_start(raw(QS[ROW_SHIFT:ROW_SHIFT + 1, HQ * g:HQ * g + HQ, :]),
                             raw(NEGM[:, :])).then_inc(shift_loaded, 16)

            def load_attn(b, g, has_prev=True):
                if has_prev:
                    waits((o_taken, 4 * b + g + 1), (o_split, 2 * b - 1 + g // 2))
                else:
                    waits((o_taken, 4 * b + g + 1))
                sp.dma_start(OD[64 * (g % 2):64 * (g % 2) + 64, g // 2, :, :], OS[:, g % 2, :]
                             ).then_inc(o_loaded[g // 2], 16)

            def store(b):
                sp.dma_start(out[bass.ds(b, 1)].rearrange("o (t p) d -> p (o t) d", p=P), ACC[:, :, :]
                             ).then_inc(stored, 16)

            def store_tiles(b, half):
                sp.dma_start(out[b].rearrange("(t p) d -> p t d", p=P)[:, 2 * half:2 * half + 2, :],
                             ACC[:, 2 * half:2 * half + 2, :]).then_inc(stored, 16)

            def scores_done(units):
                waits((st_filled[1], units))

            sp.dma_start(XT[:, :, :], x[0].rearrange("(t p) d -> p t d", p=P)).then_inc(x_loaded, 16)
            for w in names:
                src = w_dram[w].rearrange("(c p) n -> p c n", p=P)
                if w == "we":
                    for r in range(4):
                        sp.dma_start(WRAW[w][:, :, DE * r:DE * r + DE], src).then_inc(w_loaded[w], 16)
                    sp.dma_start(MU[:, :, :], mu).then_inc(mu_loaded, 16)
                else:
                    sp.dma_start(WRAW[w], src).then_inc(w_loaded[w], 16)
            sp.wait_ge(fill_ready, 2)
            fill_rows = ROWS - ROW_SHIFT
            for dst, r0 in ((QS, 0), (KS, 64)):
                src = raw(FILL[r0:r0 + fill_rows, :]).rearrange("p (o s) -> p o s", o=1)
                sp.dma_start(raw(dst[ROW_SHIFT:ROWS, :, :]).rearrange("p h (r s) -> p (h r) s", s=P),
                             src.broadcast_to([fill_rows, H * S // P, P])).then_inc(filled_up, 16)
            sp.wait_ge(xn_ready, 1)
            sp.dma_start(XT[:, :, :], x[1].rearrange("(t p) d -> p t d", p=P)).then_inc(x_loaded, 16)
            for g in range(3):
                load_context_rows(0, g)
                load_head_rows(0, g)
                if g == 0:
                    load_context_operands(0, 0)
            sp.wait_ge(filled_up, 32)
            load_shift(0, 0)

            def body(b, has_prev, has_next, has_after):
                n = b + 1
                if has_prev:
                    scores_done(16 * b)
                load_context_operands(b, 1)
                load_context_rows(b, 3)
                if has_prev:
                    load_attn(b - 1, 3)
                load_head_rows(b, 3)
                load_shift(4 * b + 1, 1)
                scores_done(16 * b + 4)
                if has_next:
                    load_context_rows(n, 0)
                    load_head_rows(n, 0)
                load_attn(b, 0, has_prev)
                load_shift(4 * b + 2, 2)
                if has_prev:
                    waits((out_ready, 2 * b))
                    store(b - 1)
                scores_done(16 * b + 8)
                if has_next:
                    load_context_operands(n, 0)
                    load_context_rows(n, 1)
                    load_head_rows(n, 1)
                load_acc(b)
                load_attn(b, 1, has_prev)
                if has_after:
                    load_x(n + 1)
                load_shift(4 * b + 3, 3)
                scores_done(16 * b + 12)
                if has_next:
                    load_context_rows(n, 2)
                    load_head_rows(n, 2)
                load_attn(b, 2, has_prev)
                if has_next:
                    load_shift(4 * b + 4, 0)

            run(sp, body)
            load_attn(B - 1, 3)
            for half in range(2):
                sp.wait_ge(out_ready, 2 * B - 1 + half)
                store_tiles(B - 1, half)
            sp.wait_ge(stored, 16 * (B + 1))

        @block.tensor
        def _(pe):
            mm = nc.tensor.matmul

            def term(dst, lhs, rhs, i):
                (lh, ll), (rh, rl) = lhs, rhs
                a, c = ((lh, rl), (ll, rh), (lh, rh))[i // CT]
                return mm(dst, a(i % CT), c(i % CT), start=(i == 0), stop=(i == TERMS - 1))

            def product(dst, lhs, rhs):
                for i in range(TERMS):
                    last = term(dst, lhs, rhs, i)
                return last

            def pair(high, low, cols):
                return (lambda k: high[:, k, cols]), (lambda k: low[:, k, cols])

            def cols(i, n=P):
                return slice(i * n, i * n + n)

            every = slice(None)

            def job_transpose(n, j, bank, *free):
                pe.wait_ge(xn_ready, n + 1)
                wait_for(free)
                for t in range(TT):
                    last = nc.tensor.transpose(bank[:, cols(t)], XN[:, t, cols(j)], IDENT[:, :])
                last.then_inc(t_filled, 1)

            def job_context(n, bank, *free):
                pe.wait_ge(xn_split, 2 * n + 2)
                wait_for(free)
                product(bank, pair(WH["we"], WL["we"], every), pair(XNH, XNL, every)
                        ).then_inc(ctx_filled, 1)

            def job_qk(n, i, bank, *free):
                wait_for(free)
                w = ("wq", "wk")[i % 2]
                product(bank, pair(WH[w], WL[w], cols(i // 2)), pair(XNH, XNL, every)
                        ).then_inc(qk_filled, 1)

            def job_kf(n, j, bank, *free):
                pe.wait_ge(mix_split, 2 * n + 1)
                wait_for(free)
                product(bank, pair(WH["wkf"], WL["wkf"], cols(j)), pair(MIXH, MIXL, every)
                        ).then_inc(kf_filled, 1)

            def token_job(j, lhs, w, bank, filled):
                for i in range(2):
                    last = product(token_tiles(bank)[:, i, :], pair(*lhs, cols(2 * j + i)),
                                   pair(WH[w], WL[w], every))
                last.then_inc(filled, 1)

            def job_out(b, j, bank, *free):
                pe.wait_ge(o_split, 2 * b + 2)
                wait_for(free)
                token_job(j, (LATEH, LATEL), "wo", bank, wo_filled)

            def job_gate(n, j, bank, *free):
                pe.wait_ge(mix_split, 2 * n + 2)
                wait_for(free)
                token_job(j, (MIXH, MIXL), "wr", bank, r_filled)

            def job_vf(n, j, bank, *free):
                pe.wait_ge(kact_split, n + 1)
                wait_for(free)
                token_job(j, (LATEH, LATEL), "wvf", bank, vf_filled)

            def job_v(n, j, bank, *free):
                wait_for(free)
                token_job(j, (XNH, XNL), "wv", bank, v_filled)

            def wait_for(free):
                for s, v in free:
                    pe.wait_ge(s, v)

            def weight(w):
                pe.wait_ge(w_split, names.index(w) + 1)

            def max_piece(b, g, i):
                use = BANK_USES * (4 * b + g) + i
                if not isinstance(use, int) or use >= 2:
                    pe.wait_ge(max_taken, use - 1)
                h = HQ * g + i // TT
                mm(MAXB[:, (g + i) % 2, :], QS[0:ROW_QK2, h, cols(i % TT)], KS[0:ROW_QK2, h, :],
                   start=True, stop=True).then_inc(max_filled, 1)

            def maxima_rows(b, g):
                pe.wait_ge(ctx_rows_loaded[g], CTX_DMAS * (b + 1))
                pe.wait_ge(maxima_rows_loaded[g], MAXIMA_DMAS * (b + 1))

            def shift_rows(b, g):
                pe.wait_ge(max_taken, BANK_USES * (4 * b + g) + PIECES)
                nc.tensor.transpose(MAXB[0:PIECES, (g + PIECES) % 2, 0:P], MX[:, :], IDENT[:, :]
                                    ).then_inc(max_filled, 1)

            def exact_scores(b, g, kt, half):
                u = 16 * b + 4 * g + kt
                if kt == 0 and half == 0:
                    pe.wait_ge(ca_loaded[g // 2], CA_DMAS * (b + 1))
                    pe.wait_ge(heads_loaded[g], HEAD_DMAS * (b + 1))
                    pe.wait_ge(shift_loaded, 16 * (4 * b + g + 1))
                pe.wait_ge(exp_done[half], u)
                for j in range(2):
                    h = HQ * g + 2 * half + j
                    mm(ST[half][:, j, :], CAK[:, g // 2, cols(kt)], CAQ[:, g // 2, :],
                       start=True, stop=False)
                    last = mm(ST[half][:, j, :], KS[0:ROWS, h, cols(kt)], QS[0:ROWS, h, :],
                              start=False, stop=True)
                last.then_inc(st_filled[half], 1)

            def values(b, g, kt):
                u = 16 * b + 4 * g + kt
                if g == 0 and kt % 2 == 0:
                    pe.wait_ge(v_ready, 2 * b + kt // 2 + 1)
                if kt == 0:
                    pe.wait_ge(o_taken, 4 * b + g)
                for half in range(2):
                    pe.wait_ge(exp_done[half], u + 1)
                for j in range(HQ):
                    v = VP[:, kt, HQ * g + j, :, :].rearrange("p d w -> p (d w)")
                    last = mm(PV[32 * j:32 * j + 32, :], v, PT[:, kt % 2, j, :],
                              start=(kt == 0), stop=(kt == TT - 1))
                last.then_inc(pv_done, 1)

            pe.wait_ge(ident_ready, 1)
            for _ in range(WARM_UP):
                mm(FIRST[5][:, 0:P], IDENT[:, :], IDENT[:, :], start=True, stop=True)
            job_transpose(0, 0, FIRST[0])
            job_transpose(0, 1, FIRST[1])
            weight("we")
            pe.wait_ge(first_high, 2)
            for i, w in enumerate((WL["we"], WH["we"])):
                for k in range(CT):
                    mm(FIRST[2], w[:, k, :], XNH[:, k, :], start=(i == k == 0), stop=False)
            pe.wait_ge(xn_split, 2)
            for k in range(CT):
                last = mm(FIRST[2], WH["we"][:, k, :], XNL[:, k, :], start=False, stop=(k == CT - 1))
            last.then_inc(ctx_filled, 1)
            weight("wq")
            job_qk(0, 0, FIRST[3])
            weight("wk")
            job_qk(0, 1, FIRST[4])
            job_qk(0, 2, FIRST[5])
            job_qk(0, 3, FIRST[0], (xnt_ready, 1), (xn_split, 1))
            weight("wv")
            job_v(0, 0, FIRST[1], (xnt_ready, 2), (xn_split, 2))
            job_v(0, 1, FIRST[3], (qk_split, 1))
            weight("wkf")
            maxima_rows(0, 0)
            for i in range(PIECES):
                max_piece(0, 0, i)
                if i >= PIECES - 2 * TERMS:
                    j, t = divmod(i - (PIECES - 2 * TERMS), TERMS)
                    if t == 0:
                        pe.wait_ge(mix_split, 1)
                        wait_for([((ctx_staged, 1), (qk_split, 2))[j]])
                    last = term(FIRST[(2, 4)[j]], pair(WH["wkf"], WL["wkf"], cols(j)),
                                pair(MIXH, MIXL, every), t)
                    if t == TERMS - 1:
                        last.then_inc(kf_filled, 1)
            shift_rows(0, 0)
            maxima_rows(0, 1)
            for i in range(HQ):
                max_piece(0, 1, i)
            pe.wait_ge(w_late_split, 3)
            pe.wait_ge(zeroed, 3)
            pe.wait_ge(qk_split, 4)
            pe.wait_ge(relu_ready, 2)
            pe.wait_ge(v_ready, 2)

            def body(b, has_prev, has_next, has_after):
                n = b + 1
                bank = JOB[:, :]

                def first_job(u):
                    if has_next:
                        if u == 1 and has_prev:
                            job_transpose(n, 0, bank, (v_ready, 2 * n))
                        if u == 1 and not has_prev:
                            job_transpose(n, 0, bank, (r_ready, 2))
                        if u == 3:
                            job_context(n, bank, (xnt_ready, 2 * n + 2))
                        if u == 6 and has_prev:
                            job_kf(n, 0, bank, (qk_split, 4 * n + 2))
                        if u == 6 and not has_prev:
                            job_kf(n, 0, bank, (vf_taken, 1))
                    if not has_prev:
                        if u == 0:
                            job_gate(0, 0, bank)
                        if u == 5:
                            job_vf(0, 0, bank, (qk_split, 4 * n + 2))
                        if u == 7:
                            job_vf(0, 1, bank, (relu_ready, 2 * n + 1))
                    if has_prev:
                        if u == 7 and has_next:
                            job_out(b - 1, 0, bank, (relu_ready, 2 * n + 1))
                        if u == 7 and not has_next:
                            job_out(b - 1, 0, bank, (v_ready, 2 * b + 2))
                    if has_next:
                        if u == 8 and has_prev:
                            job_kf(n, 1, bank, (out_ready, 2 * b))
                        if u == 8 and not has_prev:
                            job_kf(n, 1, bank, (vf_taken, 2))
                        if u == 9:
                            job_qk(n, 2, bank, (relu_ready, 2 * n + 2))
                        if u == 10:
                            job_qk(n, 3, bank, (qk_split, 4 * n + 3))
                        if u == 11:
                            job_gate(n, 1, bank, (r_ready, 2 * n + 1))
                        if u == 12:
                            job_vf(n, 0, bank, (r_ready, 2 * n + 2))
                        if u == 13:
                            job_vf(n, 1, bank, (vf_taken, 2 * n + 1))
                        if u == 14:
                            job_v(n, 0, bank, (vf_taken, 2 * n + 2))
                        if u == 15:
                            job_v(n, 1, bank, (v_ready, 2 * n + 1))

                def second_job(u):
                    if has_next:
                        if u == 4:
                            job_qk(n, 1, bank, (qk_split, 4 * n + 1))

                def third_job(u):
                    if u == 0 and not has_prev:
                        job_gate(0, 1, bank, (r_ready, 1))
                    if u == 1 and has_next:
                        job_transpose(n, 1, bank, (xnt_ready, 2 * n + 1))
                    if has_prev and u == 7:
                        job_out(b - 1, 1, bank, (out_ready, 2 * b - 1))
                    if has_next:
                        if u == 3:
                            job_qk(n, 0, bank, (ctx_staged, n + 1))
                        if u == 10:
                            job_gate(n, 0, bank, (qk_split, 4 * n + 4))

                def piece(u, i):
                    later, q, pieces = maxima_ahead(b, u)
                    if not later or has_next:
                        max_piece(b + later, q, pieces[i])

                for u in range(NU):
                    g, kt = divmod(u, TT)
                    if kt == TT - 1:
                        later, q, _ = maxima_ahead(b, u)
                        if not later or has_next:
                            maxima_rows(b + later, q)
                    exact_scores(b, g, kt, 0)
                    if kt == TT - 1 and (g < NQ - 1 or has_next):
                        shift_rows(b + (g + 1) // NQ, (g + 1) % NQ)
                    piece(u, 0)
                    if u in (2, 4) or u in (0, 5) and has_prev:
                        exact_scores(b, g, kt, 1)
                        piece(u, 1)
                        second_job(u)
                    else:
                        first_job(u)
                        piece(u, 1)
                        exact_scores(b, g, kt, 1)
                        second_job(u)
                    piece(u, 2)
                    if u > 0:
                        values(b, (u - 1) // TT, (u - 1) % TT)
                    elif has_prev:
                        values(b - 1, NQ - 1, TT - 1)
                    piece(u, 3)
                    third_job(u)

            run(pe, body)
            values(B - 1, NQ - 1, TT - 1)
            pe.wait_ge(o_split, 2 * B - 1)
            pe.wait_ge(exp_done[0], 16 * B)
            for i in range(TT):
                pe.wait_ge(last_split, i + 1)
                last = product(token_tiles(FIRST[2 + i // 2])[:, i % 2, :], pair(LATEH, LATEL, cols(i)),
                               pair(WH["wo"], WL["wo"], every))
                if i % 2:
                    last.then_inc(wo_filled, 1)

        @block.scalar
        def _(act):
            A = nc.scalar.activation

            def exps(b, g, kt, half):
                u = 16 * b + 4 * g + kt
                if half == 0 and (not isinstance(u, int) or u > 1):
                    act.wait_ge(pv_done, u - 1)
                act.wait_ge(st_filled[half], u + 1)
                A(PT[:, kt % 2, 2 * half:2 * half + 2, :], ST[half][:, :, :], ACT.Exp
                  ).then_inc(exp_done[half], 1)

            def take_attn(b, g):
                act.wait_ge(pv_done, 16 * b + 4 * (g + 1))
                if g >= 2:
                    act.wait_ge(o_loaded[0], O_DMAS * (2 * b + 2))
                else:
                    act.wait_ge(o_loaded[1], O_DMAS * (2 * b))
                A(OS[:, g % 2, :], PV[:, :], ACT.Copy).then_inc(o_taken, 1)

            def take_transpose(n, j, bank=JOB[:, :]):
                if j == 0:
                    act.wait_ge(mix_split, 2 * n)
                    act.wait_ge(xn_split, 2 * n)
                act.wait_ge(t_filled, 2 * n + j + 1)
                if j == 0:
                    act.wait_ge(v_filled, 2 * n)
                A(XNH[:, j, :], bank, ACT.Copy)
                A(XNT[:, j, 1:], bank, ACT.Copy).then_inc(xnt_ready, 1)

            def scale_before(n, i):
                act.wait_ge(xnt_ready, 2 * n + 2)
                act.wait_ge(mix_split, 2 * n + i)
                for c in range(CT):
                    A(MIX[:, c, :], XNT[:, c, 0:S], ACT.Copy, scale=OMM[:, i, c:c + 1]
                      ).then_inc(mix_scaled, 1)

            def mix_highs(n, i):
                if i == 0:
                    act.wait_ge(r_filled, 2 * n)
                else:
                    act.wait_ge(kf_filled, 2 * n + 2)
                act.wait_ge(mix_ready, 4 * n + 2 * i + 2)
                A(MIXH[:, :, :], MIX[:, :, :], ACT.Copy).then_inc(mix_high, 1)

            def kact_highs(n, b=None):
                if b is not None:
                    act.wait_ge(wo_filled, 2 * b)
                act.wait_ge(kact_ready, 2 * n + 2)
                A(LATEH[:, :, :], KACT, ACT.Copy).then_inc(kact_high, 1)

            def qk_highs(n, i, bank=JOB[:, :]):
                act.wait_ge(qk_filled, 4 * n + i + 1)
                if i % 2 == 0:
                    for g in (i, i + 1):
                        act.wait_ge(maxima_rows_loaded[g], MAXIMA_DMAS * n)
                        act.wait_ge(heads_loaded[g], HEAD_DMAS * n)
                A((QH, KH)[i % 2][:, i // 2, :], bank, ACT.Copy, scale=(SCALE, 1.0)[i % 2]
                  ).then_inc(qk_high, 1)

            def relus(n, j, bank=JOB[:, :]):
                act.wait_ge(kf_filled, 2 * n + j + 1)
                act.wait_ge(t_filled, 2 * n + 2)
                A(KACT[:, j, :], bank, ACT.Relu).then_inc(relu_ready, 1)

            def context_highs(n, bank=JOB[:, :]):
                act.wait_ge(ctx_filled, n + 1)
                for g in range(NQ):
                    act.wait_ge(ctx_rows_loaded[g], CTX_DMAS * n)
                for i in range(2):
                    act.wait_ge(ca_loaded[i], CA_DMAS * n)
                A(CTX[0:2 * DE, :], bank[0:2 * DE, :], ACT.Copy, scale=FACTOR[0:2 * DE, :]).then_inc(ctx_high, 1)

            def gates(n, j, bank=JOB[:, :]):
                act.wait_ge(r_filled, 2 * n + j + 1)
                act.wait_ge(acc_ready, 2 * n)
                A(R[:, 2 * j:2 * j + 2, :], token_tiles(bank), ACT.Tanh, scale=0.5).then_inc(r_ready, 1)

            def take_values(n, j, has_prev=True, bank=JOB[:, :]):
                act.wait_ge(v_filled, 2 * n + j + 1)
                if has_prev:
                    act.wait_ge(pv_done, 16 * n - 2 + 2 * j)
                A(VP[:, 2 * j:2 * j + 2, :, :, 0],
                  token_tiles(bank).rearrange("p i (h d) -> p i h d", h=H), ACT.Copy).then_inc(v_ready, 1)

            def weight_high(w):
                act.wait_ge(w_loaded[w], 16 * (4 if w == "we" else 1))
                if w == "wvf":
                    A(WRAW[w], WRAW[w], ACT.Copy, scale=0.5).then_inc(w_halved, 1)
                    act.wait_ge(w_halved, 1)
                A(WH[w][:, :, :], WRAW[w], ACT.Copy).then_inc(w_high, 1)

            for w in ("we", "wq", "wk"):
                weight_high(w)
            act.wait_ge(zeroed, 1)
            for j in range(CT):
                act.wait_ge(t_filled, j + 1)
                A(XNH[:, j, :], FIRST[j], ACT.Copy).then_inc(first_high, 1)
            for j in range(CT):
                act.wait_ge(xn_split, j + 1)
                A(XNT[:, j, 1:], FIRST[j], ACT.Copy).then_inc(xnt_ready, 1)
            weight_high("wv")
            act.wait_ge(mu_ready, 1)
            context_highs(0, FIRST[2])
            qk_highs(0, 0, FIRST[3])
            weight_high("wkf")
            qk_highs(0, 1, FIRST[4])
            scale_before(0, 0)
            qk_highs(0, 2, FIRST[5])
            mix_highs(0, 0)
            qk_highs(0, 3, FIRST[0])
            act.wait_ge(ones_ready, 1)
            take_values(0, 0, False, FIRST[1])
            take_values(0, 1, False, FIRST[3])
            for w in names[5:]:
                weight_high(w)
            scale_before(0, 1)
            relus(0, 0, FIRST[2])
            relus(0, 1, FIRST[4])
            mix_highs(0, 1)
            kact_highs(0)

            def body(b, has_prev, has_next, has_after):
                n = b + 1

                def after_first(u):
                    if not has_prev and u == 0:
                        gates(0, 0)
                    if has_next:
                        if u == 1:
                            take_transpose(n, 0)
                        if u == 11:
                            gates(n, 1)
                        if u == 2:
                            scale_before(n, 0)
                        if u == 3:
                            context_highs(n)
                        if u == 6:
                            relus(n, 0)
                        if u == 8:
                            relus(n, 1)
                        if 9 <= u < 11:
                            qk_highs(n, u - 7)

                def after_second(u):
                    if has_prev and u == 0:
                        take_values(b, 1)
                    if not has_prev and u == 0:
                        gates(0, 1)
                    if has_next:
                        if u == 1:
                            take_transpose(n, 1)
                        if u == 4:
                            qk_highs(n, 1)
                        if u == 3:
                            mix_highs(n, 0)
                        if u == 7:
                            scale_before(n, 1)
                        if u == 9:
                            mix_highs(n, 1)
                            kact_highs(n, b if has_prev else None)
                        if u == 10:
                            gates(n, 0)
                        if u == 14:
                            take_values(n, 0)

                for u in range(NU):
                    g, kt = divmod(u, TT)
                    if u == 4 and has_next:
                        qk_highs(n, 0)
                    exps(b, g, kt, 0)
                    after_first(u)
                    exps(b, g, kt, 1)
                    after_second(u)
                    if kt == 0 and g > 0:
                        take_attn(b, g - 1)
                    elif u == 0 and has_prev:
                        take_attn(b - 1, NQ - 1)

            run(act, body)
            take_attn(B - 1, NQ - 1)

        @block.vector
        def _(dve):
            V = nc.vector

            def row_maximum(b, g, i):
                dve.wait_ge(max_filled, BANK_USES * (4 * b + g) + i + 1)
                V.reduce_max(MX[:, i:i + 1], MAXB[:, (g + i) % 2, :], AX.X).then_inc(max_taken, 1)

            def take_shift(b, g):
                q = 4 * b + g
                dve.wait_ge(max_filled, BANK_USES * (q + 1))
                dve.wait_ge(shift_loaded, 16 * q)
                V.tensor_scalar(NEGM[:, :], MAXB[0:PIECES, (g + PIECES) % 2, 0:P], -1.0, None, ALU.mult
                                ).then_inc(max_taken, 1)

            def layernorm_stats(n, half):
                if half == 0:
                    dve.wait_ge(x_loaded, 16 * (n + 1))
                for t in range(2 * half, 2 * half + 2):
                    last = V.bn_stats(STATS[:, t, :], XT[:, t, :])
                last.then_inc(stats_ready, 1)

            def layernorm_moments(n):
                for t in range(TT):
                    last = V.bn_aggr(MV[:, t, :], STATS[:, t, :])
                last.then_inc(mv_ready, 1)

            def layernorm(n, half):
                if half == 0:
                    dve.wait_ge(rstd_ready, n + 1)
                    dve.wait_ge(kact_split, n)
                for t in range(2 * half, 2 * half + 2):
                    last = V.tensor_scalar(XN[:, t, :], XT[:, t, :], MV[:, t, 0:1], RSTD[:, t:t + 1],
                                           ALU.subtract, ALU.mult)
                if half == 1:
                    last.then_inc(xn_ready, 1)

            def qk_lows(n, i, bank=JOB[:, :]):
                dve.wait_ge(qk_high, 4 * n + i + 1)
                high, low = ((QH, QL), (KH, KL))[i % 2]
                V.scalar_tensor_tensor(out=low[:, i // 2, :], in0=bank, scalar=(SCALE, 1.0)[i % 2],
                                       in1=raw(high[:, i // 2, :]), op0=ALU.mult, op1=ALU.subtract
                                       ).then_inc(qk_split, 1)

            def mix(n, i, c):
                dve.wait_ge(mix_scaled, 4 * n + 2 * i + c + 1)
                V.scalar_tensor_tensor(out=MIX[:, c, :], in0=XNT[:, c, 1:], scalar=MU[:, i, c:c + 1],
                                       in1=MIX[:, c, :], op0=ALU.mult, op1=ALU.add).then_inc(mix_ready, 1)

            def context_lows(n, bank=JOB[:, :]):
                dve.wait_ge(ctx_high, n + 1)
                high = raw(CTX[0:2 * DE, :])
                V.scalar_tensor_tensor(out=CTX[2 * DE:P, :], in0=bank[2 * DE:P, :], scalar=FACTOR[2 * DE:P, :],
                                       in1=high, op0=ALU.mult, op1=ALU.subtract).then_inc(ctx_staged, 1)

            def take_vf(n, j, bank=JOB[:, :]):
                r = R[:, 2 * j:2 * j + 2, :]
                dve.wait_ge(vf_filled, 2 * n + j + 1)
                dve.wait_ge(r_ready, 2 * n + j + 1)
                V.scalar_tensor_tensor(out=r, in0=r, scalar=1.0, in1=token_tiles(bank),
                                       op0=ALU.add, op1=ALU.mult).then_inc(vf_taken, 1)

            def invert_sums(b, t, i):
                if i == 0:
                    dve.wait_ge(o_loaded[t], O_DMAS * 2 * (b + 1))
                V.reciprocal(DEN[:, t, i * P:i * P + P], DEN[:, t, i * P:i * P + P]).then_inc(den_ready, 1)

            def norm_attn(b, t):
                dve.wait_ge(den_ready, TT * (2 * b + t + 1))
                V.tensor_tensor(OT[:, t, :], OT[:, t, :], DEN[:, t, :], ALU.mult).then_inc(o_normed, 1)

            def attn_highs(b, t, n=None):
                dve.wait_ge(o_normed, 2 * b + t + 1)
                if n is not None:
                    dve.wait_ge(vf_filled, 2 * n + 2)
                elif t == 0:
                    dve.wait_ge(wo_filled, 2 * b)
                V.tensor_copy(LATEH[:, t, :], OT[:, t, :]).then_inc(o_high, 1)

            def take_out(b, j, bank=JOB[:, :]):
                acc = ACC[:, 2 * j:2 * j + 2, :]
                dve.wait_ge(wo_filled, 2 * b + j + 1)
                dve.wait_ge(acc_ready, 2 * b + 2)
                V.tensor_tensor(acc, token_tiles(bank), acc, ALU.add).then_inc(out_ready, 1)

            V.memset(XNT[:, :, 0:1], 0.0)
            for i in range(P // DE):
                last = V.memset(FACTOR[DE * i:DE * i + DE, :], (1.0, INFLUENCE)[i % 2])
            last.then_inc(zeroed, 1)
            for half in range(2):
                layernorm_stats(0, half)
            dve.wait_ge(stats_ready, 2)
            layernorm_moments(0)
            V.memset(FILL[0:64, :], 0.0).then_inc(fill_ready, 1)
            V.memset(FILL[64:P, :], 1.0).then_inc(fill_ready, 1)
            for half in range(2):
                layernorm(0, half)

            def weight_low(w):
                i = names.index(w)
                dve.wait_ge(w_high, i + 1)
                V.tensor_tensor(WL[w][:, :, :], WRAW[w], raw(WH[w][:, :, :]), ALU.subtract
                                ).then_inc(w_split, 1)

            dve.wait_ge(mu_loaded, 16)
            V.tensor_scalar(OMM[:, :, :], MU[:, :, :], -1.0, 1.0, ALU.mult, ALU.add).then_inc(mu_ready, 1)
            weight_low("we")
            weight_low("wq")
            V.memset(raw(CAQ[2 * DE:P, :, :]), 0.0).then_inc(zeroed, 1)
            V.memset(raw(CAK[2 * DE:P, :, :]), 0.0).then_inc(zeroed, 1)
            for j in range(CT):
                dve.wait_ge(first_high, j + 1)
                V.tensor_tensor(XNL[:, j, :], FIRST[j], raw(XNH[:, j, :]), ALU.subtract).then_inc(xn_split, 1)
            weight_low("wk")
            weight_low("wv")
            context_lows(0, FIRST[2])
            qk_lows(0, 0, FIRST[3])
            weight_low("wkf")
            qk_lows(0, 1, FIRST[4])
            for c in range(CT):
                mix(0, 0, c)
            qk_lows(0, 2, FIRST[5])
            qk_lows(0, 3, FIRST[0])
            for i in range(PIECES):
                row_maximum(0, 0, i)
                if i in (12, 15):
                    mix(0, 1, (12, 15).index(i))
            take_shift(0, 0)
            for i in range(HQ):
                row_maximum(0, 1, i)
                if i < 2:
                    layernorm_stats(1, i)
            dve.wait_ge(stats_ready, 4)
            layernorm_moments(1)

            def body(b, has_prev, has_next, has_after):
                n = b + 1

                def between_maxima(u, at):
                    now = (u, at)
                    if has_next:
                        if now == (3, 1):
                            context_lows(n)
                        if now in ((2, 3), (3, 2)):
                            mix(n, 0, u - 2)
                        if now == (4, 3):
                            qk_lows(n, 1)
                        if now in ((8, 2), (8, 3)):
                            mix(n, 1, at - 2)
                        if now == (9, 1):
                            qk_lows(n, 2)
                        if now == (10, 1):
                            qk_lows(n, 3)
                        if now in ((12, 1), (13, 1)):
                            take_vf(n, u - 12)
                    if not has_prev and now in ((0, 0), (0, 2)):
                        layernorm(1, at // 2)
                    if not has_prev and now in ((5, 1), (7, 1)):
                        take_vf(0, (u - 5) // 2)
                    if has_prev:
                        if now in ((1, 3), (3, 3), (4, 1), (5, 3)):
                            invert_sums(b - 1, 1, (1, 3, 4, 5).index(u))
                        if now == (6, 0):
                            norm_attn(b - 1, 1)
                            attn_highs(b - 1, 1)
                        if now == (7, 0):
                            take_out(b - 1, 0)
                    if now in ((10, 3), (11, 2), (12, 3), (13, 3)):
                        invert_sums(b, 0, u - 10)
                    if now == (14, 1):
                        norm_attn(b, 0)
                    if now == (15, 0):
                        attn_highs(b, 0, n if has_next else None)
                    if has_after:
                        if now in ((11, 3), (12, 2)):
                            layernorm_stats(n + 1, u - 11)
                        if now == (13, 2):
                            layernorm_moments(n + 1)
                        if now in ((14, 3), (15, 2)):
                            layernorm(n + 1, u - 14)

                for u in range(NU):
                    g, kt = divmod(u, TT)
                    later, q, pieces = maxima_ahead(b, u)
                    if kt == TT - 1 and (g < NQ - 1 or has_next):
                        take_shift(b + (g + 1) // NQ, (g + 1) % NQ)
                    if has_next and u == 4:
                        qk_lows(n, 0)
                    if has_prev and u == 8:
                        take_out(b - 1, 1)
                    if has_after and u == 13:
                        dve.wait_ge(stats_ready, 2 * n + 4)
                    for i in range(HQ):
                        if not later or has_next:
                            row_maximum(b + later, q, pieces[i])
                        between_maxima(u, i)

            run(dve, body)

            def last_tile(i):
                tile = slice(i * P, i * P + P)
                dve.wait_ge(den_ready, TT * (2 * B - 1) + i + 1)
                V.tensor_tensor(OT[:, 1, tile], OT[:, 1, tile], DEN[:, 1, tile], ALU.mult).then_inc(last_normed, 1)
                dve.wait_ge(last_normed, i + 1)
                V.tensor_copy(LATEH[:, 1, tile], OT[:, 1, tile]).then_inc(last_high, 1)
                dve.wait_ge(last_high, i + 1)
                V.tensor_tensor(LATEL[:, 1, tile], OT[:, 1, tile], raw(LATEH[:, 1, tile]), ALU.subtract
                                ).then_inc(last_split, 1)

            for i in range(TT):
                invert_sums(B - 1, 1, i)
                if i > 0:
                    last_tile(i - 1)
                if i == TT - 1:
                    take_out(B - 1, 0, FIRST[2])
            last_tile(TT - 1)
            take_out(B - 1, 1, FIRST[3])

        @block.gpsimd
        def _(pool):
            G = nc.gpsimd

            def rstd(n):
                pool.wait_ge(mv_ready, n + 1)
                pool.wait_ge(xn_ready, n)
                G.tensor_tensor(VE[:, :], MV[:, :, 1], EPSV[:, :], ALU.add).then_inc(var_ready, 1)
                pool.wait_ge(var_ready, n + 1)
                G.tensor_tensor(RSTD[:, :], VE[:, :], HALF[:, :], ALU.pow).then_inc(rstd_ready, 1)

            def lows(ready, count, low, whole, high, done):
                pool.wait_ge(ready, count)
                G.tensor_tensor(low, whole, raw(high), ALU.subtract).then_inc(done, 1)

            def xn_lows(n):
                for j in range(CT):
                    lows(xnt_ready, 2 * n + j + 1, XNL[:, j, :], XNT[:, j, 1:], XNH[:, j, :], xn_split)

            def mix_lows(n, i):
                lows(mix_high, 2 * n + i + 1, MIXL[:, :, :], MIX[:, :, :], MIXH[:, :, :], mix_split)

            def kacts(n, c):
                pool.wait_ge(relu_ready, 2 * n + c + 1)
                G.tensor_tensor(KACT[:, c, :], KACT[:, c, :], KACT[:, c, :], ALU.mult
                                ).then_inc(kact_ready, 1)

            def kact_lows(n):
                lows(kact_high, n + 1, LATEL[:, :, :], KACT, LATEH[:, :, :], kact_split)

            def attn_lows(b, t):
                lows(o_high, 2 * b + t + 1, LATEL[:, t, :], OT[:, t, :], LATEH[:, t, :], o_split)

            def add_vf(n, j):
                pool.wait_ge(vf_taken, 2 * n + j + 1)
                pool.wait_ge(acc_loaded, 16 * (n + 1))
                acc = ACC[:, 2 * j:2 * j + 2, :]
                G.tensor_tensor(acc, acc, R[:, 2 * j:2 * j + 2, :], ALU.add).then_inc(acc_ready, 1)

            G.memset(IDENT[:, :], 0.0).then_inc(ident_zero, 1)
            pool.wait_ge(ident_zero, 1)
            G.affine_select(out=IDENT[:, :], in_=IDENT[:, :], compare_op=ALU.not_equal, fill=1.0, base=0,
                            pattern=[[-1, P]], channel_multiplier=1).then_inc(ident_ready, 1)
            G.memset(EPSV[:, :], EPS).then_inc(ident_zero, 1)
            G.memset(HALF[:, :], -0.5).then_inc(ident_zero, 1)
            pool.wait_ge(ident_zero, 3)
            rstd(0)
            G.memset(VP[:, :, :, :, :].rearrange("p t h d w -> p (t h d w)"), 1.0).then_inc(ones_ready, 1)
            mix_lows(0, 0)
            for w in names[5:]:
                lows(w_high, names.index(w) + 1, WL[w][:, :, :], WRAW[w], WH[w][:, :, :], w_late_split)
            for c in range(CT):
                kacts(0, c)
            mix_lows(0, 1)
            kact_lows(0)
            rstd(1)

            def body(b, has_prev, has_next, has_after):
                n = b + 1
                if has_next:
                    xn_lows(n)
                    mix_lows(n, 0)
                if has_prev:
                    attn_lows(b - 1, 1)
                if has_next:
                    for c in range(CT):
                        kacts(n, c)
                    mix_lows(n, 1)
                for j in range(2):
                    add_vf(b, j)
                if has_next:
                    kact_lows(n)
                if has_after:
                    rstd(n + 1)
                attn_lows(b, 0)

            run(pool, body)


_INS = ["x", "wq", "wk", "wv", "wo", "we", "wr", "wkf", "wvf", "mu"]


def kernel(L0_attn_X, L0_attn_Wq, L0_attn_Wk, L0_attn_Wv, L0_attn_Wo, L0_attn_We,
           L0_ffn_W_r, L0_ffn_W_k, L0_ffn_W_v, L0_ffn_mu_r, L0_ffn_mu_k):
    import numpy as np
    import concourse.bacc as bacc
    from concourse.bass_utils import run_bass_kernel_spmd

    def by_channel(w):
        w = np.asarray(w).T.reshape(D, H // HQ, HQ, DK)
        return np.ascontiguousarray(w.transpose(0, 1, 3, 2).reshape(D, D))

    def turned(w):
        return np.ascontiguousarray(np.asarray(w).T)

    arrays = {
        "x": np.ascontiguousarray(L0_attn_X),
        "wq": by_channel(L0_attn_Wq), "wk": by_channel(L0_attn_Wk), "wv": turned(L0_attn_Wv),
        "wo": turned(L0_attn_Wo), "we": turned(L0_attn_We), "wr": turned(L0_ffn_W_r),
        "wkf": turned(L0_ffn_W_k), "wvf": turned(L0_ffn_W_v),
        "mu": np.ascontiguousarray(np.stack([L0_ffn_mu_k, L0_ffn_mu_r]).reshape(2, CT, P).transpose(2, 0, 1)),
    }
    nc = bacc.Bacc("TRN2", target_bir_lowering=False, num_devices=1)
    args = [nc.dram_tensor(f"in_{k}", arrays[k].shape, mybir.dt.from_np(arrays[k].dtype),
                           kind="ExternalInput").ap() for k in _INS]
    out = nc.dram_tensor("out_0", (B, S, D), F32, kind="ExternalOutput").ap()
    block_kernel(nc, *args, out)
    r = run_bass_kernel_spmd(nc, [{f"in_{k}": arrays[k] for k in _INS}], core_ids=[0])
    return r.results[0]["out_0"]
```
